# Optimizing a Trainium2 kernel written in Bass

```python
import numpy as np
import jax
import jax.numpy as jnp

def _softmax(x, axis=-1):
    return jax.nn.softmax(x, axis=axis)

def _gelu(x):
    return jax.nn.gelu(x, approximate=True)

def _silu(x):
    return jax.nn.silu(x)

def _sigmoid(x):
    return jax.nn.sigmoid(x)

def _layernorm(x, axis=-1, eps=1e-05):
    m = jnp.mean(x, axis=axis, keepdims=True)
    v = jnp.var(x, axis=axis, keepdims=True)
    return (x - m) / jnp.sqrt(v + eps)

def _scatter_add(tgt, idx, src, axis=0):
    return tgt.at[idx].add(src)

def _segment_sum(src, seg, n):
    return jax.ops.segment_sum(src, seg, n)
kernel_name = 'mk_recurrent_d1_jaxref_r8_d65e1a'

def setup_inputs(seed: int=0):
    np.random.seed(seed)
    _w = jnp.asarray

    def _L0_attn_setup():
        import jax, jax.numpy as jnp
        import numpy as np
        HEADS = 64
        DIM_HEAD = 64
        SCALE = DIM_HEAD ** (-0.5)
        EPS = 1e-06
        key = jax.random.key(seed)
        ks = jax.random.split(key, 6)
        b, s, dim = (2, 512, 128)
        inner = HEADS * DIM_HEAD
        std = 0.02
        return {'x': jax.random.normal(ks[0], (b, s, dim), dtype=jnp.float32), 'Wq': jax.random.normal(ks[1], (dim, inner), dtype=jnp.float32) * std, 'Wk': jax.random.normal(ks[2], (dim, inner), dtype=jnp.float32) * std, 'Wv': jax.random.normal(ks[3], (dim, inner), dtype=jnp.float32) * std, 'Wo': jax.random.normal(ks[4], (inner, dim), dtype=jnp.float32) * std, 'bo': jnp.zeros((dim,), dtype=jnp.float32)}
    _L0_attn_in = _L0_attn_setup()

    def _L0_ffn_setup():
        import jax, jax.numpy as jnp
        import numpy as np
        DIM = 128
        DEPTH = 2
        HEADS = 8
        DIM_HEAD = 64
        WINDOW = 64
        INNER = HEADS * DIM_HEAD
        HID = int(DIM * 4 * 2 / 3)
        B, N = (2, 1024)
        QK_SCALE = 8.0

        def shift_token(t):
            t1, t2 = jnp.split(t, 2, axis=-1)
            t2 = jnp.pad(t2, ((0, 0), (1, 0), (0, 0)))[:, :-1]
            return jnp.concatenate([t1, t2], axis=-1)

        def l2norm(t):
            return t / jnp.clip(jnp.linalg.norm(t, axis=-1, keepdims=True), 1e-12)

        def rotate_half(x):
            x1, x2 = jnp.split(x, 2, axis=-1)
            return jnp.concatenate([-x2, x1], axis=-1)

        def rotary_xpos(q, k):
            n = q.shape[-2]
            half_idx = jnp.arange(0, DIM_HEAD, 2, dtype=jnp.float32)
            inv_freq = 1.0 / 10000.0 ** (half_idx / DIM_HEAD)
            t = jnp.arange(n, dtype=jnp.float32)
            freqs = t[:, None] * inv_freq[None, :]
            freqs = jnp.concatenate([freqs, freqs], axis=-1)
            base = (half_idx + 0.4 * DIM_HEAD) / (1.4 * DIM_HEAD)
            power = (t - n // 2) / float(WINDOW // 2)
            scale = base[None, :] ** power[:, None]
            scale = jnp.concatenate([scale, scale], axis=-1)
            cos, sin = (jnp.cos(freqs), jnp.sin(freqs))
            q = q * cos * scale + rotate_half(q) * sin * scale
            k = k * cos / scale + rotate_half(k) * sin / scale
            return (q, k)

        def local_attention(q, k, v):
            b, h, n, d = q.shape
            w = n // WINDOW
            bq = q.reshape(b, h, w, WINDOW, d) * QK_SCALE
            bk = k.reshape(b, h, w, WINDOW, d)
            bv = v.reshape(b, h, w, WINDOW, d)

            def look_around(t):
                p = jnp.pad(t, ((0, 0), (0, 0), (1, 0), (0, 0), (0, 0)))
                return jnp.concatenate([p[:, :, :w], p[:, :, 1:]], axis=3)
            bk, bv = (look_around(bk), look_around(bv))
            bt = jnp.arange(n).reshape(w, WINDOW)
            btp = jnp.pad(bt, ((1, 0), (0, 0)), constant_values=-1)
            btk = jnp.concatenate([btp[:w], btp[1:]], axis=1)
            sim = jnp.einsum('bhwid,bhwjd->bhwij', bq, bk)
            i = bt[:, :, None]
            j = btk[:, None, :]
            mask = (i < j) | (i > j + WINDOW) | (j == -1)
            sim = jnp.where(mask, -jnp.finfo(sim.dtype).max, sim)
            attn = jax.nn.softmax(sim, axis=-1)
            out = jnp.einsum('bhwij,bhwjd->bhwid', attn, bv)
            return out.reshape(b, h, n, d)

        def _layer(x, wqkv, qs, ksc, wo, lg, lb, w1, b1, w2, b2):
            b, n, _ = x.shape
            h = shift_token(x)
            qkv = h @ wqkv
            q, k, v = jnp.split(qkv, 3, axis=-1)
            to_heads = lambda t: t.reshape(b, n, HEADS, DIM_HEAD).transpose(0, 2, 1, 3)
            q, k, v = (to_heads(q), to_heads(k), to_heads(v))
            q = l2norm(q) * qs
            k = l2norm(k) * ksc
            q, k = rotary_xpos(q, k)
            o = local_attention(q, k, v)
            o = o.transpose(0, 2, 1, 3).reshape(b, n, INNER)
            x = x + o @ wo
            h = shift_token(x)
            mu = h.mean(-1, keepdims=True)
            var = h.var(-1, keepdims=True)
            h = (h - mu) / jnp.sqrt(var + 1e-05) * lg + lb
            h = h @ w1 + b1
            a, g = jnp.split(h, 2, axis=-1)
            h = a * jax.nn.gelu(g, approximate=False)
            x = x + h @ w2 + b2
            return x
        key = jax.random.key(seed)
        ks = jax.random.split(key, 6)
        return {'x': jax.random.normal(ks[0], (B, N, DIM), jnp.float32), 'wqkv': jax.random.normal(ks[1], (DEPTH, DIM, 3 * INNER), jnp.float32) * 0.02, 'q_scale': jnp.ones((DEPTH, DIM_HEAD), jnp.float32), 'k_scale': jnp.ones((DEPTH, DIM_HEAD), jnp.float32), 'wo': jax.random.normal(ks[2], (DEPTH, INNER, DIM), jnp.float32) * 0.02, 'ln_g': jnp.ones((DEPTH, DIM), jnp.float32), 'ln_b': jnp.zeros((DEPTH, DIM), jnp.float32), 'w1': jax.random.normal(ks[3], (DEPTH, DIM, 2 * HID), jnp.float32) * 0.02, 'b1': jnp.zeros((DEPTH, 2 * HID), jnp.float32), 'w2': jax.random.normal(ks[4], (DEPTH, HID, DIM), jnp.float32) * 0.02, 'b2': jnp.zeros((DEPTH, DIM), jnp.float32)}
    _L0_ffn_in = _L0_ffn_setup()
    _d = {'L0_attn_x': _L0_attn_in['x'], 'L0_attn_Wq': _L0_attn_in['Wq'], 'L0_attn_Wk': _L0_attn_in['Wk'], 'L0_attn_Wv': _L0_attn_in['Wv'], 'L0_attn_Wo': _L0_attn_in['Wo'], 'L0_attn_bo': _L0_attn_in['bo'], 'L0_ffn_wqkv': _L0_ffn_in['wqkv'], 'L0_ffn_q_scale': _L0_ffn_in['q_scale'], 'L0_ffn_k_scale': _L0_ffn_in['k_scale'], 'L0_ffn_wo': _L0_ffn_in['wo'], 'L0_ffn_ln_g': _L0_ffn_in['ln_g'], 'L0_ffn_ln_b': _L0_ffn_in['ln_b'], 'L0_ffn_w1': _L0_ffn_in['w1'], 'L0_ffn_b1': _L0_ffn_in['b1'], 'L0_ffn_w2': _L0_ffn_in['w2'], 'L0_ffn_b2': _L0_ffn_in['b2']}
    _x0 = _d['L0_attn_x']
    _d['L0_attn_x'] = jax.random.normal(jax.random.fold_in(jax.random.key(seed), 1), (4, 512, 128), dtype=_x0.dtype)
    del _x0
    return _d

def reference(L0_attn_x, L0_attn_Wq, L0_attn_Wk, L0_attn_Wv, L0_attn_Wo, L0_attn_bo, L0_ffn_wqkv, L0_ffn_q_scale, L0_ffn_k_scale, L0_ffn_wo, L0_ffn_ln_g, L0_ffn_ln_b, L0_ffn_w1, L0_ffn_b1, L0_ffn_w2, L0_ffn_b2):

    def _L0_attn_ref(x, Wq, Wk, Wv, Wo, bo):
        import jax, jax.numpy as jnp
        import numpy as np
        HEADS = 64
        DIM_HEAD = 64
        SCALE = DIM_HEAD ** (-0.5)
        EPS = 1e-06
        b, s, dim = x.shape
        h, dh = (HEADS, DIM_HEAD)
        q = (x @ Wq).reshape(b, s, h, dh)
        k = (x @ Wk).reshape(b, s, h, dh)
        v = (x @ Wv).reshape(b, s, h, dh)
        q = jax.nn.relu(q) * SCALE
        k = jax.nn.relu(k)
        kv = jnp.einsum('bsid,bsjd->bsdj', k, v)
        out = jnp.einsum('bsid,bsdj->bsij', q, kv)
        q_norm = jnp.einsum('bsid,bsd->bsi', q, k.sum(axis=2))
        out = out / (q_norm[..., None] + EPS)
        out = out.reshape(b, s, h * h)
        return out @ Wo + bo

    def _L0_ffn_ref(x, wqkv, q_scale, k_scale, wo, ln_g, ln_b, w1, b1, w2, b2):
        import jax, jax.numpy as jnp
        import numpy as np
        DIM = 128
        DEPTH = 2
        HEADS = 8
        DIM_HEAD = 64
        WINDOW = 64
        INNER = HEADS * DIM_HEAD
        HID = int(DIM * 4 * 2 / 3)
        B, N = (2, 1024)
        QK_SCALE = 8.0

        def shift_token(t):
            t1, t2 = jnp.split(t, 2, axis=-1)
            t2 = jnp.pad(t2, ((0, 0), (1, 0), (0, 0)))[:, :-1]
            return jnp.concatenate([t1, t2], axis=-1)

        def l2norm(t):
            return t / jnp.clip(jnp.linalg.norm(t, axis=-1, keepdims=True), 1e-12)

        def rotate_half(x):
            x1, x2 = jnp.split(x, 2, axis=-1)
            return jnp.concatenate([-x2, x1], axis=-1)

        def rotary_xpos(q, k):
            n = q.shape[-2]
            half_idx = jnp.arange(0, DIM_HEAD, 2, dtype=jnp.float32)
            inv_freq = 1.0 / 10000.0 ** (half_idx / DIM_HEAD)
            t = jnp.arange(n, dtype=jnp.float32)
            freqs = t[:, None] * inv_freq[None, :]
            freqs = jnp.concatenate([freqs, freqs], axis=-1)
            base = (half_idx + 0.4 * DIM_HEAD) / (1.4 * DIM_HEAD)
            power = (t - n // 2) / float(WINDOW // 2)
            scale = base[None, :] ** power[:, None]
            scale = jnp.concatenate([scale, scale], axis=-1)
            cos, sin = (jnp.cos(freqs), jnp.sin(freqs))
            q = q * cos * scale + rotate_half(q) * sin * scale
            k = k * cos / scale + rotate_half(k) * sin / scale
            return (q, k)

        def local_attention(q, k, v):
            b, h, n, d = q.shape
            w = n // WINDOW
            bq = q.reshape(b, h, w, WINDOW, d) * QK_SCALE
            bk = k.reshape(b, h, w, WINDOW, d)
            bv = v.reshape(b, h, w, WINDOW, d)

            def look_around(t):
                p = jnp.pad(t, ((0, 0), (0, 0), (1, 0), (0, 0), (0, 0)))
                return jnp.concatenate([p[:, :, :w], p[:, :, 1:]], axis=3)
            bk, bv = (look_around(bk), look_around(bv))
            bt = jnp.arange(n).reshape(w, WINDOW)
            btp = jnp.pad(bt, ((1, 0), (0, 0)), constant_values=-1)
            btk = jnp.concatenate([btp[:w], btp[1:]], axis=1)
            sim = jnp.einsum('bhwid,bhwjd->bhwij', bq, bk)
            i = bt[:, :, None]
            j = btk[:, None, :]
            mask = (i < j) | (i > j + WINDOW) | (j == -1)
            sim = jnp.where(mask, -jnp.finfo(sim.dtype).max, sim)
            attn = jax.nn.softmax(sim, axis=-1)
            out = jnp.einsum('bhwij,bhwjd->bhwid', attn, bv)
            return out.reshape(b, h, n, d)

        def _layer(x, wqkv, qs, ksc, wo, lg, lb, w1, b1, w2, b2):
            b, n, _ = x.shape
            h = shift_token(x)
            qkv = h @ wqkv
            q, k, v = jnp.split(qkv, 3, axis=-1)
            to_heads = lambda t: t.reshape(b, n, HEADS, DIM_HEAD).transpose(0, 2, 1, 3)
            q, k, v = (to_heads(q), to_heads(k), to_heads(v))
            q = l2norm(q) * qs
            k = l2norm(k) * ksc
            q, k = rotary_xpos(q, k)
            o = local_attention(q, k, v)
            o = o.transpose(0, 2, 1, 3).reshape(b, n, INNER)
            x = x + o @ wo
            h = shift_token(x)
            mu = h.mean(-1, keepdims=True)
            var = h.var(-1, keepdims=True)
            h = (h - mu) / jnp.sqrt(var + 1e-05) * lg + lb
            h = h @ w1 + b1
            a, g = jnp.split(h, 2, axis=-1)
            h = a * jax.nn.gelu(g, approximate=False)
            x = x + h @ w2 + b2
            return x
        for l in range(DEPTH):
            x = _layer(x, wqkv[l], q_scale[l], k_scale[l], wo[l], ln_g[l], ln_b[l], w1[l], b1[l], w2[l], b2[l])
        return x
    x = L0_attn_x
    xn = _layernorm(x, axis=-1)
    s = _L0_attn_ref(xn, L0_attn_Wq, L0_attn_Wk, L0_attn_Wv, L0_attn_Wo, L0_attn_bo)
    g = _silu(_L0_ffn_ref(xn, L0_ffn_wqkv, L0_ffn_q_scale, L0_ffn_k_scale, L0_ffn_wo, L0_ffn_ln_g, L0_ffn_ln_b, L0_ffn_w1, L0_ffn_b1, L0_ffn_w2, L0_ffn_b2))
    x = x + s * g
    return x

_drawn_inputs = setup_inputs


def setup_inputs(seed=0):
    import zlib

    import numpy as np

    out = dict(_drawn_inputs(seed))
    spreads = {'L0_attn_bo': (0.0, 0.1),
     'L0_ffn_q_scale': (1.0, 0.6),
     'L0_ffn_k_scale': (1.0, 0.6),
     'L0_ffn_ln_g': (1.0, 0.6),
     'L0_ffn_ln_b': (0.0, 0.8),
     'L0_ffn_b1': (0.0, 0.8),
     'L0_ffn_b2': (0.0, 0.793)}
    factors = {'L0_attn_Wk': 8.0,
     'L0_ffn_wqkv': 8.0,
     'L0_ffn_wo': 8.0,
     'L0_ffn_w1': 8.0,
     'L0_ffn_w2': 8.0}
    for name, (base, spread) in spreads.items():
        noise = np.random.default_rng([zlib.crc32(name.encode()), seed]).standard_normal(out[name].shape)
        drawn = base * np.exp(spread * noise) if base else spread * noise
        out[name] = jnp.asarray(drawn.astype(out[name].dtype))
    for name, factor in factors.items():
        out[name] = (out[name] * factor).astype(out[name].dtype)
    return out
```

```python
import concourse.bass as bass
from concourse import mybir
from contextlib import ExitStack

FP32 = mybir.dt.float32
I32 = mybir.dt.int32
ALU = mybir.AluOpType
ACT = mybir.ActivationFunctionType
AX_X = mybir.AxisListType.X

BATCH, SEQ, DIM = 4, 512, 128
TOKENS = BATCH * SEQ
P = 128
LH, LD = 64, 64
LSCALE = LD ** -0.5
LEPS = 1e-6
DEPTH, FH, FD, WIN = 2, 8, 64, 64
INNER = FH * FD
HID = int(DIM * 4 * 2 / 3)
QK_SCALE = 8.0
LN_EPS = 1e-5
NORM_FLOOR_SQ = 1e-24
MASKED = -1e30
RSQRT_GUESS = 0x5F3759DF + 1
CT = 64
CHUNKS = TOKENS // (2 * CT)
HALF = P // 2
QT = SEQ // P
UNITS = DEPTH * BATCH
HID_TILES = [(f * P, min(P, HID - f * P)) for f in range(-(-HID // P))]
KEYS = WIN + P


def head_of(slot):
    return 4 * (slot // 4) + (slot // 2) % 2 + 2 * (slot % 2)


def nth(i, per_turn, k=0):
    return i * per_turn + k + 1


def wait_alone(engine, semaphore, value):
    engine.wait_ge(semaphore, value)
    engine.nop(nofuse=True)


RSQRT_STEPS = 11


def rsqrt(nc, dve, y, x, work, stepped, before):
    steps = [lambda: nc.vector.tensor_scalar(work.bitcast(I32), x.bitcast(I32), 1, -1,
                                             ALU.logical_shift_right, ALU.bitwise_xor),
             lambda: nc.vector.tensor_scalar(y.bitcast(I32), work.bitcast(I32), RSQRT_GUESS, None, ALU.add)]
    for _ in range(3):
        steps += [lambda: nc.vector.scalar_tensor_tensor(out=work, in0=y, scalar=-0.5, in1=y,
                                                         op0=ALU.mult, op1=ALU.mult),
                  lambda: nc.vector.tensor_tensor(work, work, x, ALU.mult),
                  lambda: nc.vector.scalar_tensor_tensor(out=y, in0=work, scalar=1.5, in1=y,
                                                         op0=ALU.add, op1=ALU.mult)]
    for k, step in enumerate(steps):
        step().then_inc(stepped, 1)
        dve.wait_ge(stepped, before + k + 1)


def build(nc, x, wq, wk, wv, wo, bo, wqkv, q_scale, k_scale, fwo, ln_g, ln_b,
          w1, b1, w2, b2, rot, out):
    with ExitStack() as ctx:
        def sb(name, shape, scope=ctx):
            return scope.enter_context(nc.sbuf_tensor(name, shape, FP32))

        def sem(name):
            return ctx.enter_context(nc.semaphore(name))

        keep = {
            "x_tok": sb("x_tok", [P, CHUNKS, DIM]),
            "xn_t": sb("xn_t", [P, TOKENS]),
            "res": sb("res", [P, BATCH, SEQ]),
            "gate": sb("gate", [P, CHUNKS, DIM]),
            "ident": sb("ident", [P, P]),
            "wq": sb("wq_sb", [P, LH * LD]),
            "wk": sb("wk_sb", [P, LH * LD]),
            "wv": sb("wv_sb", [P, LH * LD]),
            "psum": ctx.enter_context(nc.psum_tensor("psum", [P, 8, 512], FP32)),
            "lin_w_in": sem("lin_w_in"),
        }
        normalise_input(nc, keep, x)
        gate_branch(nc, keep, wqkv, q_scale, k_scale, fwo, ln_g, ln_b, w1, b1, w2, b2, rot,
                    (wq, wk, wv))
        linear_branch(nc, keep, wo, bo, out)


def normalise_input(nc, keep, x):
    x_tok, xn_t, res, ident, psum = (keep[n] for n in ("x_tok", "xn_t", "res", "ident", "psum"))
    x_by_chunk = x.rearrange("b t d -> (b t) d").rearrange("(h c s) d -> h s c d", h=2, s=CT)
    with ExitStack() as ctx:
        def sb(name, shape):
            return ctx.enter_context(nc.sbuf_tensor(name, shape, FP32))

        def sem(name):
            return ctx.enter_context(nc.semaphore(name))

        xc = sb("xc", [P, CHUNKS, DIM])
        xsq = sb("xsq", [P, CHUNKS, DIM])
        stat = sb("stat", [P, 4, CHUNKS])
        x_in = sem("x_in")
        ident_zero, ident_ready = sem("ident_zero"), sem("ident_ready")
        stat_step, rsqrt_step = sem("stat_step"), sem("input_rsqrt_step")
        centred, squared, xn_ready = sem("centred"), sem("squared"), sem("xn_ready")
        turned, xn_t_ready = sem("turned"), sem("xn_t_ready")
        block = ctx.enter_context(nc.Block())

        def per_token(row):
            return stat[:, row, :].unsqueeze(2).broadcast_to([P, CHUNKS, DIM])

        @block.sync
        def _(sp):
            for h in range(2):
                sp.dma_start(x_tok[h * HALF:(h + 1) * HALF, :, :], x_by_chunk[h]).then_inc(x_in, 16)

        @block.gpsimd
        def _(pool):
            nc.gpsimd.memset(ident[:, :], 0.0).then_inc(ident_zero, 1)
            pool.wait_ge(ident_zero, 1)
            nc.gpsimd.affine_select(out=ident[:, :], in_=ident[:, :], compare_op=ALU.not_equal, fill=1.0,
                                    base=0, pattern=[[-1, P]], channel_multiplier=1).then_inc(ident_ready, 1)

        @block.vector
        def _(dve):
            dve.wait_ge(x_in, 32)
            nc.vector.reduce_sum(stat[:, 0, :], x_tok[:, :, :], AX_X).then_inc(stat_step, 1)
            dve.wait_ge(stat_step, 1)
            nc.vector.tensor_scalar(stat[:, 1, :], stat[:, 0, :], 1.0 / DIM, None, ALU.mult).then_inc(stat_step, 1)
            dve.wait_ge(stat_step, 2)
            nc.vector.tensor_tensor(xc[:, :, :], x_tok[:, :, :], per_token(1), ALU.subtract).then_inc(centred, 1)
            dve.wait_ge(squared, 1)
            nc.vector.reduce_sum(stat[:, 2, :], xsq[:, :, :], AX_X).then_inc(stat_step, 1)
            dve.wait_ge(stat_step, 3)
            nc.vector.tensor_scalar(stat[:, 3, :], stat[:, 2, :], 1.0 / DIM, LN_EPS, ALU.mult, ALU.add) \
                .then_inc(stat_step, 1)
            dve.wait_ge(stat_step, 4)
            rsqrt(nc, dve, stat[:, 0, :], stat[:, 3, :], stat[:, 1, :], rsqrt_step, 0)
            nc.vector.tensor_tensor(xc[:, :, :], xc[:, :, :], per_token(0), ALU.mult).then_inc(xn_ready, 1)

        @block.scalar
        def _(act):
            act.wait_ge(centred, 1)
            nc.scalar.activation(xsq[:, :, :], xc[:, :, :], ACT.Square).then_inc(squared, 1)
            by_chunk = xn_t[:, :].rearrange("p (h c s) -> p c h s", h=2, s=CT)
            for g in range(CHUNKS // 4):
                act.wait_ge(turned, g + 1)
                src = psum[:, g, :].rearrange("p (c h s) -> p c h s", c=4, h=2)
                nc.scalar.activation(by_chunk[:, 4 * g:4 * g + 4], src, ACT.Copy).then_inc(xn_t_ready, 1)
            act.wait_ge(xn_t_ready, CHUNKS // 4)
            nc.scalar.activation(res[:, :, :].rearrange("p b t -> p (b t)"), xn_t[:, :], ACT.Copy) \
                .then_inc(xn_t_ready, 1)

        @block.tensor
        def _(pe):
            pe.wait_ge(ident_ready, 1)
            pe.wait_ge(xn_ready, 1)
            for c in range(CHUNKS):
                turn = nc.tensor.transpose(psum[:, c // 4, (c % 4) * P:(c % 4 + 1) * P], xc[:, c, :], ident[:, :])
                if c % 4 == 3:
                    turn.then_inc(turned, 1)


def gate_branch(nc, keep, wqkv, q_scale, k_scale, fwo, ln_g, ln_b, w1, b1, w2, b2, rot, lin_w):
    res, gate, ident, psum = (keep[n] for n in ("res", "gate", "ident", "psum"))
    with ExitStack() as ctx:
        def sb(name, shape):
            return ctx.enter_context(nc.sbuf_tensor(name, shape, FP32))

        def sem(name):
            return ctx.enter_context(nc.semaphore(name))

        wqkv_sb = sb("wqkv_sb", [P, 3 * INNER])
        fwo_sb = sb("fwo_sb", [P, INNER // P, DIM])
        w1_sb = sb("w1_sb", [P, 2 * HID])
        w2_sb = sb("w2_sb", [P, len(HID_TILES), DIM])
        qk_gain = sb("qk_gain", [P, 2, FD])
        lng_sb, lnb_sb, b2_sb = sb("lng_sb", [P, 1]), sb("lnb_sb", [P, 1]), sb("b2_sb", [P, 1])
        b1_sb = sb("b1_sb", [P, 2, len(HID_TILES)])
        rot_sb = sb("rot_sb", [P, 2, 2, QT, FD])
        rot_gain = sb("rot_gain", [P, 2, 2, QT, FD])
        mean_w = sb("mean_w", [P, P])
        mask = sb("mask", [P, 2, KEYS])
        h_t = sb("h_t", [P, SEQ])
        v_tok = sb("v_tok", [P, QT, INNER])
        k_t = sb("k_t", [P, FH // 2, WIN + SEQ])
        o_t = sb("o_t", [P, FH // 2, SEQ])
        qk_sq = sb("qk_sq", [P, 2 * FH, FD])
        qk_n = sb("qk_n", [P, 2 * FH, FD])
        qk_cos = sb("qk_cos", [P, 2 * FH, FD])
        qk_sin = sb("qk_sin", [P, 2 * FH, FD])
        qk_rot = sb("qk_rot", [P, 2 * FH, FD])
        q_t = sb("q_t", [P, FH // 2, P])
        qk_stat = sb("qk_stat", [P, 4, 2 * FH])
        s_mask = sb("s_mask", [P, FH, KEYS])
        prob = sb("prob", [P, FH, 2 * P])
        s_stat = sb("s_stat", [P, 4, FH])
        p_own = sb("p_own", [P, FH, P])
        p_prev = sb("p_prev", [P, FH, P])
        h2 = sb("h2", [P, SEQ])
        hc = sb("hc", [P, SEQ])
        hsq = sb("hsq", [P, SEQ])
        rstd = sb("rstd", [P, SEQ])
        std = sb("std", [P, SEQ])
        var = sb("var", [P, SEQ])
        hn = sb("hn", [P, SEQ])
        gelu = sb("gelu", [P, len(HID_TILES), SEQ])
        ffn = sb("ffn", [P, len(HID_TILES), SEQ])

        tab_in, w_in = sem("tab_in"), sem("w_in")
        consts = sem("consts")
        gain_ready = sem("gain_ready")
        h_ready, qkv_ready = sem("h_ready"), sem("qkv_ready")
        sq_ready, v_ready, ss_ready, floor_ready = sem("sq_ready"), sem("v_ready"), sem("ss_ready"), sem("floor_ready")
        qkn_ready, cos_ready, sin_ready, rot_ready = (sem("qkn_ready"), sem("cos_ready"),
                                                      sem("sin_ready"), sem("rot_ready"))
        qk_turned, qkt_ready = sem("qk_turned"), sem("qkt_ready")
        sim_ready, masked_ready, max_ready, negmax_ready = (sem("sim_ready"), sem("masked_ready"),
                                                            sem("max_ready"), sem("negmax_ready"))
        exp_ready, rsum_ready, prob_ready = sem("exp_ready"), sem("rsum_ready"), sem("prob_ready")
        p_turned, pown_ready, pprev_ready = sem("p_turned"), sem("pown_ready"), sem("pprev_ready")
        pv_ready, ot_ready, wo_ready = sem("pv_ready"), sem("ot_ready"), sem("wo_ready")
        res_mid, h2_ready, mean_ready, hc_ready = sem("res_mid"), sem("h2_ready"), sem("mean_ready"), sem("hc_ready")
        hsq_ready, var_ready, rstd_ready, hn_ready = (sem("hsq_ready"), sem("var_ready"),
                                                      sem("rstd_ready"), sem("hn_ready"))
        hidden_ready, hln_ready, gelu_ready, ffn_ready = (sem("hidden_ready"), sem("hln_ready"),
                                                          sem("gelu_ready"), sem("ffn_ready"))
        rsqrt_step, std_ready, refine = sem("rsqrt_step"), sem("std_ready"), sem("refine")
        var_kept = sem("var_kept")
        w2_ready, unit_done = sem("w2_ready"), sem("unit_done")
        silu_ready, gate_turned, gate_ready = sem("silu_ready"), sem("gate_turned"), sem("gate_ready")
        block = ctx.enter_context(nc.Block())

        NF = len(HID_TILES)
        LAYER_DMAS = 2 + 1 + NF + 2 + 3 + 2 * NF
        G_BANK = [6, 0, 1]
        A_BANK = [3, 4, 5]

        @block.sync
        def _(sp):
            sp.dma_start(rot_sb[:, :, :, :, :].rearrange("p a b t d -> p (a b t d)"), rot).then_inc(tab_in, 16)
            with sp.Fori(0, DEPTH) as layer:
                sp.wait_ge(unit_done, nth(layer, BATCH, BATCH - 1))

                def load(dst, src):
                    sp.dma_start(dst, src).then_inc(w_in, 16)

                load(wqkv_sb[:, :], wqkv[layer])
                for n, scale in enumerate((q_scale, k_scale)):
                    load(qk_gain[:, n, :], scale[layer].partition_broadcast(P))
                load(fwo_sb[:, :, :], fwo[layer].rearrange("(c p) n -> p c n", p=P))
                load(w1_sb[:, :], w1[layer])
                for f, (f0, m) in enumerate(HID_TILES):
                    load(w2_sb[0:m, f, :], w2[layer][f0:f0 + m, :])
                    for part in range(2):
                        load(b1_sb[0:m, part, f:f + 1],
                             b1[layer][part * HID + f0:part * HID + f0 + m].unsqueeze(1))
                for dst, src in ((lng_sb, ln_g), (lnb_sb, ln_b), (b2_sb, b2)):
                    load(dst[:, :], src[layer].unsqueeze(1))
            for dst, src in zip(("wk", "wv", "wq"), (lin_w[1], lin_w[2], lin_w[0])):
                sp.dma_start(keep[dst][:, :], src).then_inc(keep["lin_w_in"], 16)

        @block.gpsimd
        def _(pool):
            nc.gpsimd.memset(mean_w[:, :], 1.0 / DIM).then_inc(consts, 1)
            nc.gpsimd.memset(k_t[:, :, 0:WIN], 0.0).then_inc(consts, 1)
            nc.gpsimd.memset(prob[:, :, 0:WIN], 0.0).then_inc(consts, 1)
            nc.gpsimd.memset(mask[:, :, :], 0.0).then_inc(consts, 1)
            pool.wait_ge(consts, 4)
            nc.gpsimd.affine_select(out=mask[:, :, :], in_=mask[:, :, :], compare_op=ALU.is_ge, fill=MASKED,
                                    base=0, pattern=[[0, 2], [1, KEYS]], channel_multiplier=-1).then_inc(consts, 1)
            pool.wait_ge(consts, 5)
            nc.gpsimd.affine_select(out=mask[:, :, :], in_=mask[:, :, :], compare_op=ALU.is_ge, fill=MASKED,
                                    base=WIN, pattern=[[0, 2], [-1, KEYS]], channel_multiplier=1).then_inc(consts, 1)
            pool.wait_ge(consts, 6)
            nc.gpsimd.memset(mask[:, 0, 0:WIN], MASKED).then_inc(consts, 1)

            with pool.Fori(0, UNITS) as u:
                for t in range(QT):
                    def rotate(t):
                        pool.wait_ge(qkn_ready, nth(u, QT, t))
                        for half in range(2):
                            to = slice(half * 32, half * 32 + 32)
                            of = slice(32 - half * 32, 64 - half * 32)
                            table = rot_gain[:, 1, :, t, to].unsqueeze(2).broadcast_to([P, 2, FH, 32])
                            part = nc.gpsimd.tensor_tensor(
                                qk_sin[:, :, to].rearrange("p (a h) d -> p a h d", a=2),
                                qk_n[:, :, of].rearrange("p (a h) d -> p a h d", a=2), table, ALU.mult)
                        part.then_inc(sin_ready, 1)

                    if t == 0:
                        rotate(0)
                    if t + 1 < QT:
                        rotate(t + 1)
                    pool.wait_ge(rsum_ready, nth(u, QT, t))
                    nc.gpsimd.tensor_tensor(prob[:, :, WIN:], prob[:, :, WIN:],
                                            s_stat[:, 3, :].unsqueeze(2).broadcast_to([P, FH, KEYS]),
                                            ALU.mult).then_inc(prob_ready, 1)

        @block.scalar
        def _(act):
            act.wait_ge(consts, 7)

            def square_and_values(u, t):
                act.wait_ge(qkv_ready, nth(u, QT, t))
                nc.scalar.activation(qk_sq[:, :, :].rearrange("p h d -> p (h d)"),
                                     psum[:, 0:2, :].rearrange("p a n -> p (a n)"), ACT.Square).then_inc(sq_ready, 1)
                nc.scalar.activation(v_tok[:, t, :], psum[:, 2, :], ACT.Copy).then_inc(v_ready, 1)

            def keep_turned_qk(u, t):
                act.wait_ge(qk_turned, nth(u, QT, t))
                nc.scalar.activation(q_t[:, :, :].rearrange("p h n -> p (h n)"), psum[:, 0, :], ACT.Copy)
                nc.scalar.activation(k_t[:, :, WIN + t * P:WIN + (t + 1) * P],
                                     psum[:, 1, :].rearrange("p (h n) -> p h n", n=P), ACT.Copy).then_inc(qkt_ready, 1)

            with act.Fori(0, DEPTH) as layer:
                wait_alone(act, w_in, nth(layer, LAYER_DMAS * 16, LAYER_DMAS * 16 - 1))
                with act.Fori(0, BATCH) as b:
                    u = layer * BATCH + b
                    square_and_values(u, 0)
                    keep_turned_qk(u, 0)
                    for t in range(QT):
                        if t + 1 < QT:
                            square_and_values(u, t + 1)
                        act.wait_ge(negmax_ready, nth(u, QT, t))
                        for s in range(FH):
                            e = nc.scalar.activation(prob[:, s, WIN:], s_mask[:, s, :], ACT.Exp,
                                                     bias=s_stat[:, 1, s:s + 1], scale=QK_SCALE,
                                                     accum_out=s_stat[:, 2, s:s + 1])
                        e.then_inc(exp_ready, 1)
                        if t + 1 < QT:
                            keep_turned_qk(u, t + 1)
                        act.wait_ge(p_turned, nth(u, QT, t))
                        nc.scalar.activation(p_own[:, :, :].rearrange("p h n -> p (h n)"),
                                             psum[:, 3:5, :].rearrange("p a n -> p (a n)"), ACT.Copy) \
                            .then_inc(pown_ready, 1)
                    act.wait_ge(hc_ready, nth(u, 1))
                    nc.scalar.activation(hsq[:, :], hc[:, :], ACT.Square).then_inc(hsq_ready, 1)
                    act.wait_ge(var_kept, nth(u, 1))
                    nc.scalar.activation(std[:, :], var[:, :], ACT.Sqrt).then_inc(std_ready, 1)
                    act.wait_ge(hn_ready, nth(u, 1))
                    nc.scalar.activation(h2[:, :], hn[:, :], ACT.Identity, bias=lnb_sb[:, 0:1],
                                         scale=lng_sb[:, 0:1]).then_inc(hln_ready, 1)
                    for f, (f0, m) in enumerate(HID_TILES):
                        act.wait_ge(hidden_ready, nth(u, NF, f))
                        nc.scalar.activation(gelu[0:m, f, :], psum[0:m, G_BANK[f], :], ACT.Gelu,
                                             bias=b1_sb[0:m, 1, f:f + 1]).then_inc(gelu_ready, 1)
            act.wait_ge(unit_done, BATCH + UNITS)
            by_chunk = res[:, :, :].rearrange("p b t -> p (b t)").rearrange("p (h c s) -> p c h s", h=2, s=CT)
            chunks = v_tok[:, :, :].rearrange("p b t -> p (b t)").rearrange("p (c h s) -> p c h s", h=2, s=CT)
            nc.scalar.activation(chunks, by_chunk, ACT.Silu).then_inc(silu_ready, 1)
            for g in range(CHUNKS // 4):
                act.wait_ge(gate_turned, g + 1)
                nc.scalar.activation(gate[:, 4 * g:4 * g + 4, :].rearrange("p c n -> p (c n)"), psum[:, g, :],
                                     ACT.Copy).then_inc(gate_ready, 1)

        @block.vector
        def _(dve):
            dve.nop().then_inc(unit_done, BATCH)
            dve.wait_ge(tab_in, 16)
            dve.wait_ge(consts, 7)

            def shift_into(dst, src):
                nc.vector.tensor_copy(dst[0:HALF, :], src[0:HALF])
                nc.vector.memset(dst[HALF:P, 0:1], 0.0)
                return nc.vector.tensor_copy(dst[HALF:P, 1:SEQ], src[HALF:P, 0:SEQ - 1])

            def norm_and_rotate(u, t):
                dve.wait_ge(sq_ready, nth(u, QT, t))
                nc.vector.reduce_sum(qk_stat[:, 0, :], qk_sq[:, :, :], AX_X).then_inc(ss_ready, 1)
                dve.wait_ge(ss_ready, nth(u, QT, t))
                nc.vector.tensor_scalar(qk_stat[:, 2, :], qk_stat[:, 0, :], NORM_FLOOR_SQ, None, ALU.max) \
                    .then_inc(floor_ready, 1)
                dve.wait_ge(floor_ready, nth(u, QT, t))
                rsqrt(nc, dve, qk_stat[:, 1, :], qk_stat[:, 2, :], qk_stat[:, 3, :], rsqrt_step,
                      (u * QT + t) * RSQRT_STEPS)
                nc.vector.tensor_tensor(qk_n[:, :, :], psum[:, 0:2, :].rearrange("p a (h d) -> p (a h) d", d=FD),
                                        qk_stat[:, 1, :].unsqueeze(2).broadcast_to([P, 2 * FH, FD]),
                                        ALU.mult).then_inc(qkn_ready, 1)
                dve.wait_ge(qkn_ready, nth(u, QT, t))
                table = rot_gain[:, 0, :, t, :].unsqueeze(2).broadcast_to([P, 2, FH, FD])
                nc.vector.tensor_tensor(qk_cos[:, :, :].rearrange("p (a h) d -> p a h d", a=2),
                                        qk_n[:, :, :].rearrange("p (a h) d -> p a h d", a=2), table,
                                        ALU.mult).then_inc(cos_ready, 1)
                dve.wait_ge(cos_ready, nth(u, QT, t))
                dve.wait_ge(sin_ready, nth(u, QT, t))
                nc.vector.tensor_tensor(qk_rot[:, :, :], qk_cos[:, :, :], qk_sin[:, :, :], ALU.add) \
                    .then_inc(rot_ready, 1)

            with dve.Fori(0, DEPTH) as layer:
                dve.wait_ge(w_in, nth(layer, LAYER_DMAS * 16, LAYER_DMAS * 16 - 1))
                for n in range(2):
                    gain = qk_gain[:, n, :].unsqueeze(1)
                    nc.vector.tensor_tensor(rot_gain[:, 0, n], rot_sb[:, 0, n], gain.broadcast_to([P, QT, FD]), ALU.mult)
                    for half in range(2):
                        to = slice(half * 32, half * 32 + 32)
                        of = slice(32 - half * 32, 64 - half * 32)
                        last = nc.vector.tensor_tensor(rot_gain[:, 1, n, :, to], rot_sb[:, 1, n, :, to],
                                                       gain[:, :, of].broadcast_to([P, QT, 32]), ALU.mult)
                last.then_inc(gain_ready, 1)
                wait_alone(dve, gain_ready, layer + 1)
                with dve.Fori(0, BATCH) as b:
                    u = layer * BATCH + b
                    shift_into(h_t, res[:, b, :]).then_inc(h_ready, 1)
                    norm_and_rotate(u, 0)
                    for t in range(QT):
                        dve.wait_ge(sim_ready, nth(u, QT, t))
                        banks = psum[:, 3:7, 0:2 * KEYS].rearrange("p a (h k) -> p a h k", k=KEYS)
                        nc.vector.tensor_tensor(
                            s_mask[:, :, :].rearrange("p (a h) k -> p a h k", h=2), banks,
                            mask[:, min(t, 1), :].unsqueeze(1).unsqueeze(1).broadcast_to([P, 4, 2, KEYS]),
                            ALU.add).then_inc(masked_ready, 1)
                        dve.wait_ge(masked_ready, nth(u, QT, t))
                        nc.vector.reduce_max(s_stat[:, 0, :], s_mask[:, :, :], AX_X).then_inc(max_ready, 1)
                        dve.wait_ge(max_ready, nth(u, QT, t))
                        nc.vector.tensor_scalar(s_stat[:, 1, :], s_stat[:, 0, :], -QK_SCALE, None, ALU.mult) \
                            .then_inc(negmax_ready, 1)
                        if t + 1 < QT:
                            norm_and_rotate(u, t + 1)
                        dve.wait_ge(exp_ready, nth(u, QT, t))
                        nc.vector.reciprocal(s_stat[:, 3, :], s_stat[:, 2, :]).then_inc(rsum_ready, 1)
                        if t > 0:
                            dve.wait_ge(p_turned, nth(u, QT, t))
                            nc.vector.tensor_copy(p_prev[:, :, :].rearrange("p h n -> p (h n)"),
                                                  psum[:, 5:7, :].rearrange("p a n -> p (a n)")) \
                                .then_inc(pprev_ready, 1)
                        dve.wait_ge(pv_ready, nth(u, QT, t))
                        nc.vector.tensor_copy(o_t[:, :, t * P:(t + 1) * P],
                                              psum[:, 7, :].rearrange("p (h n) -> p h n", n=P)).then_inc(ot_ready, 1)
                    dve.wait_ge(wo_ready, nth(u, 1))
                    nc.vector.tensor_tensor(res[:, b, :], res[:, b, :], psum[:, 2, :], ALU.add).then_inc(res_mid, 1)
                    wait_alone(dve, res_mid, nth(u, 1))
                    shift_into(h2, res[:, b, :]).then_inc(h2_ready, 1)
                    dve.wait_ge(mean_ready, nth(u, 1))
                    nc.vector.tensor_tensor(hc[:, :], h2[:, :], psum[:, 0, :], ALU.subtract).then_inc(hc_ready, 1)
                    dve.wait_ge(var_ready, nth(u, 1))
                    nc.vector.tensor_scalar(var[:, :], psum[:, 1, :], LN_EPS, None, ALU.add).then_inc(var_kept, 1)
                    dve.wait_ge(std_ready, nth(u, 1))
                    nc.vector.reciprocal(rstd[:, :], std[:, :]).then_inc(refine, 1)
                    dve.wait_ge(refine, nth(u, 3))
                    nc.vector.scalar_tensor_tensor(out=std[:, :], in0=rstd[:, :], scalar=-0.5, in1=rstd[:, :],
                                                   op0=ALU.mult, op1=ALU.mult).then_inc(refine, 1)
                    dve.wait_ge(refine, nth(u, 3, 1))
                    nc.vector.tensor_tensor(std[:, :], std[:, :], var[:, :], ALU.mult).then_inc(refine, 1)
                    dve.wait_ge(refine, nth(u, 3, 2))
                    nc.vector.scalar_tensor_tensor(out=rstd[:, :], in0=std[:, :], scalar=1.5, in1=rstd[:, :],
                                                   op0=ALU.add, op1=ALU.mult).then_inc(rstd_ready, 1)
                    dve.wait_ge(rstd_ready, nth(u, 1))
                    nc.vector.tensor_tensor(hn[:, :], hc[:, :], rstd[:, :], ALU.mult).then_inc(hn_ready, 1)
                    for f, (f0, m) in enumerate(HID_TILES):
                        dve.wait_ge(gelu_ready, nth(u, NF, f))
                        nc.vector.scalar_tensor_tensor(out=ffn[0:m, f, :], in0=psum[0:m, A_BANK[f], :],
                                                       scalar=b1_sb[0:m, 0, f:f + 1], in1=gelu[0:m, f, :],
                                                       op0=ALU.add, op1=ALU.mult).then_inc(ffn_ready, 1)
                    dve.wait_ge(w2_ready, nth(u, 1))
                    nc.vector.scalar_tensor_tensor(out=res[:, b, :], in0=psum[:, 2, :], scalar=b2_sb[:, 0:1],
                                                   in1=res[:, b, :], op0=ALU.add, op1=ALU.add).then_inc(unit_done, 1)
                    wait_alone(dve, unit_done, nth(u, 1) + BATCH)

        @block.tensor
        def _(pe):
            pe.wait_ge(consts, 7)

            def project(u, t):
                if t:
                    pe.wait_ge(v_ready, nth(u, QT, t - 1))
                    pe.wait_ge(qkt_ready, nth(u, QT, t - 1))
                for n in range(3):
                    last = nc.tensor.matmul(psum[:, n, :], h_t[:, t * P:(t + 1) * P],
                                            wqkv_sb[:, n * INNER:(n + 1) * INNER], start=True, stop=True)
                last.then_inc(qkv_ready, 1)

            def turn_qk(u, t):
                pe.wait_ge(rot_ready, nth(u, QT, t))
                for n in range(2):
                    for pair in range(FH // 2):
                        pairs = qk_rot[:, n * FH + 2 * pair:n * FH + 2 * pair + 2, :]
                        last = nc.tensor.transpose(psum[:, n, pair * P:(pair + 1) * P],
                                                   pairs.rearrange("p h d -> p (h d)"), ident[:, :])
                last.then_inc(qk_turned, 1)

            with pe.Fori(0, DEPTH) as layer:
                wait_alone(pe, w_in, nth(layer, LAYER_DMAS * 16, LAYER_DMAS * 16 - 1))
                with pe.Fori(0, BATCH) as b:
                    u = layer * BATCH + b
                    pe.wait_ge(h_ready, nth(u, 1))
                    project(u, 0)
                    turn_qk(u, 0)
                    for t in range(QT):
                        pe.wait_ge(qkt_ready, nth(u, QT, t))
                        for s in range(FH):
                            h = head_of(s)
                            rows = slice((h % 2) * HALF, (h % 2 + 1) * HALF)
                            last = nc.tensor.matmul(psum[:, 3 + s // 2, (s % 2) * KEYS:(s % 2 + 1) * KEYS],
                                                    q_t[rows, h // 2, :], k_t[rows, h // 2, t * P:t * P + KEYS],
                                                    start=True, stop=True)
                        last.then_inc(sim_ready, 1)
                        if t + 1 < QT:
                            project(u, t + 1)
                            turn_qk(u, t + 1)
                        pe.wait_ge(prob_ready, nth(u, QT, t))
                        for s in range(FH):
                            last = nc.tensor.transpose(psum[:, 3 + s // 4, (s % 4) * P:(s % 4 + 1) * P],
                                                       prob[:, s, P:2 * P], ident[:, :])
                            if t:
                                last = nc.tensor.transpose(psum[:, 5 + s // 4, (s % 4) * P:(s % 4 + 1) * P],
                                                           prob[:, s, 0:P], ident[:, :])
                        last.then_inc(p_turned, 1)
                        pe.wait_ge(pown_ready, nth(u, QT, t))
                        if t:
                            pe.wait_ge(pprev_ready, nth(u, QT - 1, t - 1))
                            pe.wait_ge(ot_ready, nth(u, QT, t - 1))
                        for s in range(FH):
                            h = head_of(s)
                            o = psum[(h % 2) * HALF:(h % 2 + 1) * HALF, 7, (h // 2) * P:(h // 2 + 1) * P]
                            last = nc.tensor.matmul(o, v_tok[:, t, h * FD:(h + 1) * FD], p_own[:, s, :],
                                                    start=True, stop=(t == 0))
                            if t:
                                last = nc.tensor.matmul(o, v_tok[:, t - 1, h * FD:(h + 1) * FD], p_prev[:, s, :],
                                                        start=False, stop=True)
                        last.then_inc(pv_ready, 1)
                    pe.wait_ge(ot_ready, nth(u, QT, QT - 1))
                    for pair in range(FH // 2):
                        last = nc.tensor.matmul(psum[:, 2, :], fwo_sb[:, pair, :], o_t[:, pair, :],
                                                start=(pair == 0), stop=(pair == FH // 2 - 1))
                    last.then_inc(wo_ready, 1)
                    pe.wait_ge(h2_ready, nth(u, 1))
                    nc.tensor.matmul(psum[:, 0, :], mean_w[:, :], h2[:, :], start=True, stop=True).then_inc(mean_ready, 1)
                    pe.wait_ge(hsq_ready, nth(u, 1))
                    nc.tensor.matmul(psum[:, 1, :], mean_w[:, :], hsq[:, :], start=True, stop=True).then_inc(var_ready, 1)
                    pe.wait_ge(hln_ready, nth(u, 1))
                    for f, (f0, m) in enumerate(HID_TILES):
                        nc.tensor.matmul(psum[0:m, G_BANK[f], :], w1_sb[:, HID + f0:HID + f0 + m], h2[:, :],
                                         start=True, stop=True)
                        nc.tensor.matmul(psum[0:m, A_BANK[f], :], w1_sb[:, f0:f0 + m], h2[:, :],
                                         start=True, stop=True).then_inc(hidden_ready, 1)
                    for f, (f0, m) in enumerate(HID_TILES):
                        pe.wait_ge(ffn_ready, nth(u, NF, f))
                        last = nc.tensor.matmul(psum[:, 2, :], w2_sb[0:m, f, :], ffn[0:m, f, :],
                                                start=(f == 0), stop=(f == NF - 1))
                    last.then_inc(w2_ready, 1)
            pe.wait_ge(silu_ready, 1)
            chunks = v_tok[:, :, :].rearrange("p b (c n) -> p (b c) n", n=P)
            for c in range(CHUNKS):
                last = nc.tensor.transpose(psum[:, c // 4, (c % 4) * P:(c % 4 + 1) * P], chunks[:, c, :], ident[:, :])
                if c % 4 == 3:
                    last.then_inc(gate_turned, 1)


def linear_branch(nc, keep, wo, bo, out):
    x_tok, xn_t, gate, psum = (keep[n] for n in ("x_tok", "xn_t", "gate", "psum"))
    wq_sb, wk_sb, wv_sb, lin_w_in = keep["wq"], keep["wk"], keep["wv"], keep["lin_w_in"]
    PAIRS = LH // 2
    GROUP = 8
    NG = PAIRS // GROUP
    NT = CT // GROUP
    SLOTS = 3
    USES = [("k", g) for g in range(NG)] + [("v", g) for g in range(NG)] + [("sum", 0)] \
        + [("q", g) for g in range(NG)] + [("out", g) for g in range(NT)]
    assert len(USES) % SLOTS == 0
    PER = {"k": NG, "v": NG, "sum": 1, "q": NG, "out": NT}

    with ExitStack() as ctx:
        def sb(name, shape):
            return ctx.enter_context(nc.sbuf_tensor(name, shape, FP32))

        def sem(name):
            return ctx.enter_context(nc.semaphore(name))

        wo_sb = sb("wo_sb", [P, PAIRS, DIM])
        bo_sb = sb("bo_sb", [P, DIM])
        pair_sum = sb("pair_sum", [P, 2, HALF])
        x_chunk = sb("x_chunk", [P, 2, CT])
        k_acc = sb("k_acc", [P, GROUP, P])
        k_heads = sb("k_heads", [P, P])
        k_sum = sb("k_sum", [P, P])
        q_s = sb("q_s", [P, CT, LH])
        v_s = sb("v_s", [P, CT, LH + 2])
        denom = sb("denom", [P, 2, GROUP])
        o_s = sb("o_s", [P, PAIRS, P])
        y_sb = sb("y_sb", [P, DIM])
        y_step = sb("y_step", [P, 2, DIM])
        o_tok = sb("o_tok", [P, CHUNKS, DIM])

        wo_in, consts = sem("lin_wo_in"), sem("lin_consts")
        x_ready = sem("lin_x_ready")
        filled = {kind: sem(f"{kind}_filled") for kind in PER}
        read = {kind: sem(f"{kind}_read") for kind in PER}
        k_part, k_heads_ready, k_sum_ready = sem("k_part"), sem("k_heads_ready"), sem("k_sum_ready")
        denom_ready, recip_ready = sem("denom_ready"), sem("recip_ready")
        y_filled, y_ready, y_used, y_chain = sem("y_filled"), sem("y_ready"), sem("y_used"), sem("y_chain")
        o_ready, stored = sem("o_ready"), sem("stored")
        block = ctx.enter_context(nc.Block())

        def slot(kind, g):
            first = 2 * (USES.index((kind, g)) % SLOTS)
            return psum[:, first:first + 2, :].rearrange("p a (n c) -> p (a n) c", c=P)

        @block.sync
        def _(sp):
            rows = wo.rearrange("(ia ib ja jb) n -> jb ib ia ja n", ia=LH // 2, ib=2, ja=LH // 2, jb=2)
            for jb in range(2):
                for ib in range(2):
                    p0 = jb * HALF + ib * 32
                    sp.dma_start(wo_sb[p0:p0 + 32, :, :], rows[jb, ib]).then_inc(wo_in, 16)
            sp.dma_start(bo_sb[:, :], bo.partition_broadcast(P)).then_inc(wo_in, 16)
            out_by_chunk = out.rearrange("b t d -> (b t) d").rearrange("(h c s) d -> h c s d", h=2, s=CT)
            with sp.Fori(0, CHUNKS) as c:
                sp.wait_ge(o_ready, c + 1)
                for h in range(2):
                    sp.dma_start(out_by_chunk[h, c], o_tok[h * HALF:(h + 1) * HALF, c, :]).then_inc(stored, 16)
            sp.wait_ge(stored, CHUNKS * 2 * 16)

        @block.gpsimd
        def _(pool):
            nc.gpsimd.memset(pair_sum[:, :, :], 0.0).then_inc(consts, 1)
            nc.gpsimd.memset(v_s[:, :, LH:LH + 1], 1.0).then_inc(consts, 1)
            pool.wait_ge(consts, 2)
            for k, base in enumerate((0, -HALF)):
                nc.gpsimd.affine_select(out=pair_sum[:, :, :], in_=pair_sum[:, :, :], compare_op=ALU.not_equal,
                                        fill=1.0, base=base, pattern=[[0, 2], [-1, HALF]],
                                        channel_multiplier=1).then_inc(consts, 1)
                pool.wait_ge(consts, 3 + k)
            pool.nop().then_inc(y_used, 1)
            by_chunk = xn_t[:, :].rearrange("p (h c s) -> p c h s", h=2, s=CT)
            nc.gpsimd.tensor_copy(x_chunk[:, :, :], by_chunk[:, 0]).then_inc(x_ready, 1)
            pool.wait_ge(wo_in, 5 * 16)

            def finish(c):
                pool.wait_ge(y_ready, c + 1)
                nc.gpsimd.tensor_tensor(y_step[:, 0, :], y_sb[:, :], bo_sb[:, :], ALU.add).then_inc(y_chain, 1)
                pool.wait_ge(y_chain, nth(c, 2))
                pool.nop().then_inc(y_used, 1)
                nc.gpsimd.tensor_tensor(y_step[:, 1, :], y_step[:, 0, :], gate[:, c, :], ALU.mult).then_inc(y_chain, 1)
                pool.wait_ge(y_chain, nth(c, 2, 1))
                nc.gpsimd.tensor_tensor(o_tok[:, c, :], y_step[:, 1, :], x_tok[:, c, :], ALU.add).then_inc(o_ready, 1)

            with pool.Fori(0, CHUNKS - 1) as c:
                pool.wait_ge(filled["q"], nth(c, NG, NG - 1))
                nc.gpsimd.tensor_copy(x_chunk[:, :, :], by_chunk[:, c + 1]).then_inc(x_ready, 1)
                finish(c)
            finish(CHUNKS - 1)

        @block.scalar
        def _(act):
            act.wait_ge(consts, 4)
            with act.Fori(0, CHUNKS) as c:
                for g in range(NG):
                    act.wait_ge(filled["v"], nth(c, NG, g))
                    for half in range(2):
                        for par in range(2):
                            src = slot("v", g)[par * HALF:(par + 1) * HALF, :, half * CT:(half + 1) * CT]
                            j0 = par * PAIRS + g * GROUP
                            dst = v_s[half * HALF:(half + 1) * HALF, :, j0:j0 + GROUP].rearrange("p s j -> p j s")
                            last = nc.scalar.activation(dst, src, ACT.Copy)
                    last.then_inc(read["v"], 1)
                act.wait_ge(y_filled, c + 1)
                act.wait_ge(y_used, c + 1)
                nc.scalar.activation(y_sb[:, :], psum[:, 6, 0:DIM], ACT.Copy).then_inc(y_ready, 1)

        @block.vector
        def _(dve):
            dve.nop().then_inc(read["out"], NT)
            with dve.Fori(0, CHUNKS) as c:
                for g in range(NG):
                    dve.wait_ge(filled["k"], nth(c, NG, g))
                    if g == 0:
                        nc.vector.tensor_scalar(k_acc[:, :, :], slot("k", g), 0.0, None, ALU.max).then_inc(read["k"], 1)
                    else:
                        dve.wait_ge(read["k"], nth(c, NG, g - 1))
                        nc.vector.scalar_tensor_tensor(out=k_acc[:, :, :], in0=slot("k", g), scalar=0.0,
                                                       in1=k_acc[:, :, :], op0=ALU.max, op1=ALU.add) \
                            .then_inc(read["k"], 1)
                dve.wait_ge(read["k"], nth(c, NG, NG - 1))
                nc.vector.reduce_sum(k_heads[:, :], k_acc[:, :, :].rearrange("p n t -> p t n"), AX_X) \
                    .then_inc(k_heads_ready, 1)
                dve.wait_ge(filled["sum"], c + 1)
                nc.vector.tensor_scalar(k_sum[:, :], slot("sum", 0)[:, 0, :], LSCALE, None, ALU.mult) \
                    .then_inc(read["sum"], 1)
                dve.wait_ge(read["sum"], c + 1)
                for g in range(NG):
                    dve.wait_ge(filled["q"], nth(c, NG, g))
                    for half in range(2):
                        for par in range(2):
                            rows, toks = slice(par * HALF, (par + 1) * HALF), slice(half * CT, (half + 1) * CT)
                            i0 = par * PAIRS + g * GROUP
                            dst = q_s[half * HALF:(half + 1) * HALF, :, i0:i0 + GROUP].rearrange("p s i -> p i s")
                            last = nc.vector.scalar_tensor_tensor(
                                out=dst, in0=slot("q", g)[rows, :, toks], scalar=0.0,
                                in1=k_sum[rows, toks].unsqueeze(1).broadcast_to([HALF, GROUP, CT]),
                                op0=ALU.max, op1=ALU.mult)
                    last.then_inc(read["q"], 1)
                for g in range(NT):
                    dve.wait_ge(filled["out"], nth(c, NT, g))
                    nc.vector.tensor_scalar(denom[:, 0, :], slot("out", g)[:, :, LH], LEPS, None, ALU.add) \
                        .then_inc(denom_ready, 1)
                    dve.wait_ge(denom_ready, nth(c, NT, g))
                    nc.vector.reciprocal(denom[:, 1, :], denom[:, 0, :]).then_inc(recip_ready, 1)
                    dve.wait_ge(recip_ready, nth(c, NT, g))
                    for half in range(2):
                        for par in range(2):
                            rows = slice(half * HALF, (half + 1) * HALF)
                            s0 = half * CT + g * GROUP
                            dst = o_s[par * HALF:(par + 1) * HALF, :, s0:s0 + GROUP].rearrange("p j s -> p s j")
                            last = nc.vector.tensor_tensor(
                                dst, slot("out", g)[rows, :, par * PAIRS:(par + 1) * PAIRS],
                                denom[rows, 1, :].unsqueeze(2).broadcast_to([HALF, GROUP, PAIRS]), ALU.mult)
                    last.then_inc(read["out"], 1)

        @block.tensor
        def _(pe):
            pe.wait_ge(lin_w_in, 3 * 16)
            pe.wait_ge(wo_in, 5 * 16)
            pe.wait_ge(consts, 4)
            weights = {"k": wk_sb, "v": wv_sb, "q": wq_sb}

            with pe.Fori(0, CHUNKS) as c:
                def slot_free(kind, g):
                    n = USES.index((kind, g))
                    before, i = USES[n - SLOTS]
                    if n < SLOTS:
                        wait_alone(pe, read["out"], nth(c, NT, i))
                    elif before == "out":
                        wait_alone(pe, read["out"], nth(c, NT, i) + NT)
                    else:
                        wait_alone(pe, read[before], nth(c, PER[before], i))

                def project(kind):
                    for g in range(NG):
                        slot_free(kind, g)
                        for n in range(GROUP):
                            cols = slice((g * GROUP + n) * P, (g * GROUP + n + 1) * P)
                            last = nc.tensor.matmul(slot(kind, g)[:, n, :], weights[kind][:, cols],
                                                    x_chunk[:, :, :].rearrange("p h s -> p (h s)"),
                                                    start=True, stop=True)
                        last.then_inc(filled[kind], 1)

                pe.wait_ge(x_ready, c + 1)
                project("k")
                project("v")
                slot_free("sum", 0)
                pe.wait_ge(k_heads_ready, c + 1)
                nc.tensor.matmul(slot("sum", 0)[:, 0, :], pair_sum[:, :, :].rearrange("p a d -> p (a d)"),
                                 k_heads[:, :], start=True, stop=True).then_inc(filled["sum"], 1)
                project("q")
                pe.wait_ge(read["q"], nth(c, NG, NG - 1))
                wait_alone(pe, read["v"], nth(c, NG, NG - 1))
                for g in range(NT):
                    slot_free("out", g)
                    for n in range(GROUP):
                        for half in range(2):
                            rows = slice(half * HALF, (half + 1) * HALF)
                            last = nc.tensor.matmul(slot("out", g)[rows, n, 0:LH + 1], q_s[rows, g * GROUP + n, :],
                                                    v_s[rows, g * GROUP + n, 0:LH + 1], start=True, stop=True)
                    last.then_inc(filled["out"], 1)
                pe.wait_ge(read["out"], nth(c, NT, NT - 1) + NT)
                for n in range(PAIRS):
                    last = nc.tensor.matmul(psum[:, 6, 0:DIM], o_s[:, n, :], wo_sb[:, n, :],
                                            start=(n == 0), stop=(n == PAIRS - 1))
                last.then_inc(y_filled, 1)


def rotary_tables():
    import numpy as np
    f32 = np.float32
    half = np.arange(0, FD, 2, dtype=f32)
    inv_freq = (f32(1.0) / np.power(f32(10000.0), half / f32(FD), dtype=f32)).astype(f32)
    t = np.arange(SEQ, dtype=f32)
    freqs = t[:, None] * inv_freq[None, :]
    freqs = np.concatenate([freqs, freqs], axis=-1)
    base = (half + f32(0.4 * FD)) / f32(1.4 * FD)
    power = (t - SEQ // 2) / f32(WIN // 2)
    scale = np.power(base[None, :], power[:, None], dtype=f32)
    scale = np.concatenate([scale, scale], axis=-1)
    sign = np.where(np.arange(FD) < FD // 2, -1.0, 1.0).astype(f32)
    cos, sin = np.cos(freqs).astype(f32), np.sin(freqs).astype(f32) * sign
    tables = np.stack([np.stack([cos * scale, cos / scale]), np.stack([sin * scale, sin / scale])])
    tables = tables.reshape(2, 2, QT, P, FD).transpose(3, 0, 1, 2, 4)
    return np.ascontiguousarray(tables.reshape(P, -1).astype(f32))


_INS = ["L0_attn_x", "L0_attn_Wq", "L0_attn_Wk", "L0_attn_Wv", "L0_attn_Wo", "L0_attn_bo",
        "L0_ffn_wqkv", "L0_ffn_q_scale", "L0_ffn_k_scale", "L0_ffn_wo", "L0_ffn_ln_g", "L0_ffn_ln_b",
        "L0_ffn_w1", "L0_ffn_b1", "L0_ffn_w2", "L0_ffn_b2"]


def kernel(**inputs):
    import numpy as _np
    import concourse.bacc as _bacc
    from concourse import mybir as _mybir
    from concourse.bass_utils import run_bass_kernel_spmd as _run

    nc = _bacc.Bacc("TRN2", target_bir_lowering=False, num_devices=1)
    arrays, args = {}, []
    for name in _INS:
        a = _np.ascontiguousarray(inputs[name])
        arrays[f"in_{name}"] = a
        args.append(nc.dram_tensor(f"in_{name}", a.shape, _mybir.dt.from_np(a.dtype), kind="ExternalInput").ap())
    tables = rotary_tables()
    arrays["rotary"] = tables
    args.append(nc.dram_tensor("rotary", tables.shape, _mybir.dt.float32, kind="ExternalInput").ap())
    args.append(nc.dram_tensor("out_0", (BATCH, SEQ, DIM), _mybir.dt.float32, kind="ExternalOutput").ap())
    build(nc, *args)
    r = _run(nc, [arrays], core_ids=[0])
    return r.results[0]["out_0"]
```

```python
import concourse.bass as bass
from concourse import mybir
from contextlib import ExitStack

FP32 = mybir.dt.float32
FP16 = mybir.dt.float16
I32 = mybir.dt.int32
ALU = mybir.AluOpType
ACT = mybir.ActivationFunctionType
AX_X = mybir.AxisListType.X
REDUCE_MAX = bass.bass_isa.ReduceOp.max

BATCH, SEQ, DIM = 4, 512, 128
TOKENS = BATCH * SEQ
P = 128
LH, LD = 64, 64
LSCALE = LD ** -0.5
LEPS = 1e-6
DEPTH, FH, FD, WIN = 2, 8, 64, 64
INNER = FH * FD
HID = int(DIM * 4 * 2 / 3)
QK_SCALE = 8.0
LN_EPS = 1e-5
NORM_FLOOR_SQ = 1e-24
MASKED = -1e30
RSQRT_GUESS = 0x5F3759DF + 1
CT = 64
CHUNKS = TOKENS // (2 * CT)
HALF = P // 2
QT = SEQ // P
UNITS = DEPTH * BATCH
HID_TILES = [(f * P, min(P, HID - f * P)) for f in range(-(-HID // P))]
W_TOP = 8
K_SHIFT = 2.0 ** -(W_TOP + 7 + 6)
WORK = LH * CT + (LH + 2) * CT + LH * CT
assert WORK >= 3 * LH * LD
LANES = 2
KEYS = WIN + P


def nth(i, per_turn, k=0):
    return i * per_turn + k + 1


def wait_alone(engine, semaphore, value):
    engine.wait_ge(semaphore, value)
    engine.nop(nofuse=True)


RSQRT_STEPS = 11


def rsqrt(nc, dve, y, x, work, stepped, before):
    steps = [lambda: nc.vector.tensor_scalar(work.bitcast(I32), x.bitcast(I32), 1, -1,
                                             ALU.logical_shift_right, ALU.bitwise_xor),
             lambda: nc.vector.tensor_scalar(y.bitcast(I32), work.bitcast(I32), RSQRT_GUESS, None, ALU.add)]
    for _ in range(3):
        steps += [lambda: nc.vector.scalar_tensor_tensor(out=work, in0=y, scalar=-0.5, in1=y,
                                                         op0=ALU.mult, op1=ALU.mult),
                  lambda: nc.vector.tensor_tensor(work, work, x, ALU.mult),
                  lambda: nc.vector.scalar_tensor_tensor(out=y, in0=work, scalar=1.5, in1=y,
                                                         op0=ALU.add, op1=ALU.mult)]
    for k, step in enumerate(steps):
        step().then_inc(stepped, 1)
        dve.wait_ge(stepped, before + k + 1)


def build(nc, x, wq, wk, wv, wo, bo, wqkv, q_scale, k_scale, fwo, ln_g, ln_b,
          w1, b1, w2, b2, rot, out):
    with ExitStack() as ctx:
        def sb(name, shape, dtype=FP32, scope=ctx):
            return scope.enter_context(nc.sbuf_tensor(name, shape, dtype))

        keep = {
            "x_tok": sb("x_tok", [P, CHUNKS, DIM]),
            "xn_parts": sb("xn_parts", [P, 2, TOKENS], FP16),
            "gate": sb("gate", [P, CHUNKS, DIM]),
            "ident": sb("ident", [P, P]),
            "peak": sb("peak", [P, 4]),
            "work": sb("work", [P, WORK]),
            "psum": ctx.enter_context(nc.psum_tensor("psum", [P, 8, 512], FP32)),
            "lin_w_in": ctx.enter_context(nc.semaphore("lin_w_in")),
        }
        with ExitStack() as scope:
            keep["res"] = sb("res", [P, BATCH, SEQ], FP32, scope)
            normalise_input(nc, keep, x)
            gate_branch(nc, keep, wqkv, q_scale, k_scale, fwo, ln_g, ln_b, w1, b1, w2, b2, rot, (wq, wk, wv))
        keep["w_parts"] = sb("w_parts", [P, 3, 2, LH * LD], FP16)
        keep["scale"] = sb("scale", [P, 3, 4])
        split_weights(nc, keep)
        linear_branch(nc, keep, wo, bo, out)


def normalise_input(nc, keep, x):
    x_tok, xn_parts, res, ident, psum = (keep[n] for n in ("x_tok", "xn_parts", "res", "ident", "psum"))
    x_by_chunk = x.rearrange("b t d -> (b t) d").rearrange("(h c s) d -> h s c d", h=2, s=CT)
    with ExitStack() as ctx:
        def sb(name, shape):
            return ctx.enter_context(nc.sbuf_tensor(name, shape, FP32))

        def sem(name):
            return ctx.enter_context(nc.semaphore(name))

        xc = sb("xc", [P, CHUNKS, DIM])
        xsq = sb("xsq", [P, CHUNKS, DIM])
        stat = sb("stat", [P, 4, CHUNKS])
        x_in = sem("x_in")
        ident_zero, ident_ready = sem("ident_zero"), sem("ident_ready")
        stat_step, rsqrt_step = sem("stat_step"), sem("input_rsqrt_step")
        centred, squared, xn_ready = sem("centred"), sem("squared"), sem("xn_ready")
        turned, xn_t_ready, high_ready = sem("turned"), sem("xn_t_ready"), sem("high_ready")
        block = ctx.enter_context(nc.Block())

        def per_token(row):
            return stat[:, row, :].unsqueeze(2).broadcast_to([P, CHUNKS, DIM])

        @block.sync
        def _(sp):
            for h in range(2):
                sp.dma_start(x_tok[h * HALF:(h + 1) * HALF, :, :], x_by_chunk[h]).then_inc(x_in, 16)

        @block.gpsimd
        def _(pool):
            nc.gpsimd.memset(ident[:, :], 0.0).then_inc(ident_zero, 1)
            pool.wait_ge(ident_zero, 1)
            nc.gpsimd.affine_select(out=ident[:, :], in_=ident[:, :], compare_op=ALU.not_equal, fill=1.0,
                                    base=0, pattern=[[-1, P]], channel_multiplier=1).then_inc(ident_ready, 1)

        @block.vector
        def _(dve):
            dve.wait_ge(x_in, 32)
            nc.vector.reduce_sum(stat[:, 0, :], x_tok[:, :, :], AX_X).then_inc(stat_step, 1)
            dve.wait_ge(stat_step, 1)
            nc.vector.tensor_scalar(stat[:, 1, :], stat[:, 0, :], 1.0 / DIM, None, ALU.mult).then_inc(stat_step, 1)
            dve.wait_ge(stat_step, 2)
            nc.vector.tensor_tensor(xc[:, :, :], x_tok[:, :, :], per_token(1), ALU.subtract).then_inc(centred, 1)
            dve.wait_ge(squared, 1)
            nc.vector.reduce_sum(stat[:, 2, :], xsq[:, :, :], AX_X).then_inc(stat_step, 1)
            dve.wait_ge(stat_step, 3)
            nc.vector.tensor_scalar(stat[:, 3, :], stat[:, 2, :], 1.0 / DIM, LN_EPS, ALU.mult, ALU.add) \
                .then_inc(stat_step, 1)
            dve.wait_ge(stat_step, 4)
            rsqrt(nc, dve, stat[:, 0, :], stat[:, 3, :], stat[:, 1, :], rsqrt_step, 0)
            nc.vector.tensor_tensor(xc[:, :, :], xc[:, :, :], per_token(0), ALU.mult).then_inc(xn_ready, 1)
            dve.wait_ge(high_ready, 1)
            nc.vector.tensor_tensor(xn_parts[:, 1, :], res[:, :, :].rearrange("p b t -> p (b t)"),
                                    xn_parts[:, 0, :], ALU.subtract)

        @block.scalar
        def _(act):
            act.wait_ge(centred, 1)
            nc.scalar.activation(xsq[:, :, :], xc[:, :, :], ACT.Square).then_inc(squared, 1)
            flat = res[:, :, :].rearrange("p b t -> p (b t)")
            by_chunk = flat.rearrange("p (h c s) -> p c h s", h=2, s=CT)
            for g in range(CHUNKS // 4):
                act.wait_ge(turned, g + 1)
                src = psum[:, g, :].rearrange("p (c h s) -> p c h s", c=4, h=2)
                nc.scalar.activation(by_chunk[:, 4 * g:4 * g + 4], src, ACT.Copy).then_inc(xn_t_ready, 1)
            act.wait_ge(xn_t_ready, CHUNKS // 4)
            nc.scalar.activation(xn_parts[:, 0, :], flat, ACT.Copy).then_inc(high_ready, 1)

        @block.tensor
        def _(pe):
            pe.wait_ge(ident_ready, 1)
            pe.wait_ge(xn_ready, 1)
            for c in range(CHUNKS):
                turn = nc.tensor.transpose(psum[:, c // 4, (c % 4) * P:(c % 4 + 1) * P], xc[:, c, :], ident[:, :])
                if c % 4 == 3:
                    turn.then_inc(turned, 1)


def gate_branch(nc, keep, wqkv, q_scale, k_scale, fwo, ln_g, ln_b, w1, b1, w2, b2, rot, lin_w):
    res, gate, ident, psum = (keep[n] for n in ("res", "gate", "ident", "psum"))
    with ExitStack() as ctx:
        def sb(name, shape):
            return ctx.enter_context(nc.sbuf_tensor(name, shape, FP32))

        def sem(name):
            return ctx.enter_context(nc.semaphore(name))

        wqkv_sb = sb("wqkv_sb", [P, 3 * INNER])
        fwo_sb = sb("fwo_sb", [P, INNER // P, DIM])
        w1_sb = sb("w1_sb", [P, 2 * HID])
        w2_sb = sb("w2_sb", [P, len(HID_TILES), DIM])
        qk_gain = sb("qk_gain", [P, 2, FD])
        lng_sb, lnb_sb, b2_sb = sb("lng_sb", [P, 1]), sb("lnb_sb", [P, 1]), sb("b2_sb", [P, 1])
        b1_sb = sb("b1_sb", [P, 2, len(HID_TILES)])
        rot_sb = sb("rot_sb", [P, 2, 2, QT, FD])
        rot_gain = sb("rot_gain", [P, 2, 2, QT, FD])
        largest = sb("largest", [P, 3])
        mean_w = sb("mean_w", [P, P])
        mask = sb("mask", [P, 2, KEYS])
        h_t = sb("h_t", [P, LANES, SEQ])
        v_tok = sb("v_tok", [P, LANES, QT, INNER])
        k_t = sb("k_t", [P, LANES, FH // 2, WIN + SEQ])
        o_t = [sb("o_t", [P, FH // 2, SEQ]), gate[:, :, :].rearrange("p (n c) d -> p n (c d)", n=FH // 2)]
        qk_work = sb("qk_work", [P, 5 * 2 * INNER])
        qk_sq, qk_n, qk_cos, qk_sin, qk_rot = (
            qk_work[:, n * 2 * INNER:(n + 1) * 2 * INNER].rearrange("p (h d) -> p h d", d=FD) for n in range(5))
        q_t = sb("q_t", [P, FH, P])
        qk_stat = sb("qk_stat", [P, 4, 2 * FH])
        s_mask = sb("s_mask", [P, FH, KEYS])
        prob = sb("prob", [P, FH, 2 * P])
        s_stat = sb("s_stat", [P, 4, FH])
        p_both = sb("p_both", [P, 2, FH, P])
        p_own, p_prev = p_both[:, 0], p_both[:, 1]
        h2 = [h_t[:, l, :] for l in range(LANES)]
        spare = [qk_work, p_both[:, :, :, :].rearrange("p a h n -> p (a h n)")]
        hc, hsq, var, rstd = ([spare[l][:, n * SEQ:(n + 1) * SEQ] for l in range(LANES)] for n in range(4))
        std = hsq
        ffn = [qk_work[:, 4 * SEQ:7 * SEQ].rearrange("p (f n) -> p f n", n=SEQ),
               s_mask[:, :, :].rearrange("p h k -> p (h k)").rearrange("p (f n) -> p f n", n=SEQ)]

        tab_in, w_in = sem("tab_in"), sem("w_in")
        consts, largest_ready = sem("consts"), sem("largest_ready")
        gain_ready = sem("gain_ready")
        h_ready, qkv_ready = sem("h_ready"), sem("qkv_ready")
        sq_ready, v_ready, ss_ready, floor_ready = sem("sq_ready"), sem("v_ready"), sem("ss_ready"), sem("floor_ready")
        qkn_ready, cos_ready, sin_ready, rot_ready = (sem("qkn_ready"), sem("cos_ready"),
                                                      sem("sin_ready"), sem("rot_ready"))
        qk_turned, qkt_ready = sem("qk_turned"), sem("qkt_ready")
        sim_ready, masked_ready, max_ready, negmax_ready = (sem("sim_ready"), sem("masked_ready"),
                                                            sem("max_ready"), sem("negmax_ready"))
        exp_ready, rsum_ready, prob_ready = sem("exp_ready"), sem("rsum_ready"), sem("prob_ready")
        p_turned, pown_ready, pprev_ready = sem("p_turned"), sem("pown_ready"), sem("pprev_ready")
        pv_ready, ot_ready, wo_ready = sem("pv_ready"), sem("ot_ready"), sem("wo_ready")
        res_mid, h2_ready, mean_ready, hc_ready = sem("res_mid"), sem("h2_ready"), sem("mean_ready"), sem("hc_ready")
        hsq_ready, var_ready, rstd_ready, hn_ready = (sem("hsq_ready"), sem("var_ready"),
                                                      sem("rstd_ready"), sem("hn_ready"))
        hidden_ready, hln_ready, gelu_ready, ffn_ready = (sem("hidden_ready"), sem("hln_ready"),
                                                          sem("gelu_ready"), sem("ffn_ready"))
        rsqrt_step, std_ready, refine = sem("rsqrt_step"), sem("std_ready"), sem("refine")
        var_kept = sem("var_kept")
        w2_ready, unit_done = sem("w2_ready"), sem("unit_done")
        silu_ready, gate_turned, gate_ready = sem("silu_ready"), sem("gate_turned"), sem("gate_ready")
        block = ctx.enter_context(nc.Block())

        NF = len(HID_TILES)
        LAYER_DMAS = 2 + 1 + NF + 2 + 3 + 2 * NF
        TILES = LANES * QT
        STEPS = 2 * TILES
        HH = FH // 2
        LANE_BANK = [2, 7]
        G_BANK = [0, 3, 5]
        A_BANK = [1, 4, 6]

        def slot_bank(s):
            return 3 + 2 * (s % 2)

        def heads(s):
            return slice((s % 2) * HH, (s % 2 + 1) * HH)

        @block.sync
        def _(sp):
            sp.dma_start(rot_sb[:, :, :, :, :].rearrange("p a b t d -> p (a b t d)"), rot).then_inc(tab_in, 16)
            with sp.Fori(0, DEPTH) as layer:
                sp.wait_ge(unit_done, nth(layer, BATCH, BATCH - 1))

                def load(dst, src):
                    sp.dma_start(dst, src).then_inc(w_in, 16)

                load(wqkv_sb[:, :], wqkv[layer])
                for n, scale in enumerate((q_scale, k_scale)):
                    load(qk_gain[:, n, :], scale[layer].partition_broadcast(P))
                load(fwo_sb[:, :, :], fwo[layer].rearrange("(c p) n -> p c n", p=P))
                load(w1_sb[:, :], w1[layer])
                for f, (f0, m) in enumerate(HID_TILES):
                    load(w2_sb[0:m, f, :], w2[layer][f0:f0 + m, :])
                    for part in range(2):
                        load(b1_sb[0:m, part, f:f + 1],
                             b1[layer][part * HID + f0:part * HID + f0 + m].unsqueeze(1))
                for dst, src in ((lng_sb, ln_g), (lnb_sb, ln_b), (b2_sb, b2)):
                    load(dst[:, :], src[layer].unsqueeze(1))
            for n, src in enumerate(lin_w):
                sp.dma_start(raw_weights(keep, n), src).then_inc(keep["lin_w_in"], 16)

        @block.gpsimd
        def _(pool):
            nc.gpsimd.memset(mean_w[:, :], 1.0 / DIM).then_inc(consts, 1)
            nc.gpsimd.memset(k_t[:, :, :, 0:WIN], 0.0).then_inc(consts, 1)
            nc.gpsimd.memset(prob[:, :, 0:WIN], 0.0).then_inc(consts, 1)
            nc.gpsimd.memset(mask[:, :, :], 0.0).then_inc(consts, 1)
            nc.gpsimd.memset(q_t[:, :, :], 0.0).then_inc(consts, 1)
            pool.wait_ge(consts, 5)
            nc.gpsimd.affine_select(out=mask[:, :, :], in_=mask[:, :, :], compare_op=ALU.is_ge, fill=MASKED,
                                    base=0, pattern=[[0, 2], [1, KEYS]], channel_multiplier=-1).then_inc(consts, 1)
            pool.wait_ge(consts, 6)
            nc.gpsimd.affine_select(out=mask[:, :, :], in_=mask[:, :, :], compare_op=ALU.is_ge, fill=MASKED,
                                    base=WIN, pattern=[[0, 2], [-1, KEYS]], channel_multiplier=1).then_inc(consts, 1)
            pool.wait_ge(consts, 7)
            nc.gpsimd.memset(mask[:, 0, 0:WIN], MASKED).then_inc(consts, 1)

            with pool.Fori(0, UNITS // LANES) as u:
                def rotate(g):
                    pool.wait_ge(qkn_ready, nth(u, TILES, g))
                    for half in range(2):
                        to = slice(half * 32, half * 32 + 32)
                        of = slice(32 - half * 32, 64 - half * 32)
                        table = rot_gain[:, 1, :, g // LANES, to].unsqueeze(2).broadcast_to([P, 2, FH, 32])
                        part = nc.gpsimd.tensor_tensor(
                            qk_sin[:, :, to].rearrange("p (a h) d -> p a h d", a=2),
                            qk_n[:, :, of].rearrange("p (a h) d -> p a h d", a=2), table, ALU.mult)
                    part.then_inc(sin_ready, 1)

                def scale(s):
                    pool.wait_ge(rsum_ready, nth(u, STEPS, s))
                    nc.gpsimd.tensor_tensor(prob[:, heads(s), WIN:], prob[:, heads(s), WIN:],
                                            s_stat[:, 3, heads(s)].unsqueeze(2).broadcast_to([P, HH, KEYS]),
                                            ALU.mult).then_inc(prob_ready, 1)

                rotate(0)
                for g in range(TILES):
                    scale(2 * g)
                    if g + 1 < TILES:
                        rotate(g + 1)
                    scale(2 * g + 1)
            pool.wait_ge(largest_ready, 3)
            nc.gpsimd.partition_all_reduce(keep["peak"][:, 0:3], largest[:, :], P, REDUCE_MAX)

        @block.scalar
        def _(act):
            act.wait_ge(consts, 8)

            def square_and_values(u, g):
                act.wait_ge(qkv_ready, nth(u, TILES, g))
                nc.scalar.activation(qk_sq.rearrange("p h d -> p (h d)"),
                                     psum[:, 0:2, :].rearrange("p a n -> p (a n)"), ACT.Square).then_inc(sq_ready, 1)
                nc.scalar.activation(v_tok[:, g % LANES, g // LANES, :], psum[:, 2, :], ACT.Copy).then_inc(v_ready, 1)

            def keep_turned_qk(u, g):
                lane, t = g % LANES, g // LANES
                act.wait_ge(qk_turned, nth(u, TILES, g))
                for odd in range(2):
                    rows = slice(odd * HALF, (odd + 1) * HALF)
                    nc.scalar.activation(q_t[rows, odd::2, :], psum[rows, 0, :].rearrange("p (h n) -> p h n", n=P),
                                         ACT.Copy)
                nc.scalar.activation(k_t[:, lane, :, WIN + t * P:WIN + (t + 1) * P],
                                     psum[:, 1, :].rearrange("p (h n) -> p h n", n=P), ACT.Copy).then_inc(qkt_ready, 1)

            def exponentials(u, s):
                act.wait_ge(negmax_ready, nth(u, STEPS, s))
                for h in range(heads(s).start, heads(s).stop):
                    e = nc.scalar.activation(prob[:, h, WIN:], s_mask[:, h, :], ACT.Exp,
                                             bias=s_stat[:, 1, h:h + 1], scale=QK_SCALE,
                                             accum_out=s_stat[:, 2, h:h + 1])
                e.then_inc(exp_ready, 1)

            def keep_own(u, s):
                act.wait_ge(p_turned, nth(u, STEPS, s))
                nc.scalar.activation(p_own[:, heads(s), :].rearrange("p h n -> p (h n)"),
                                     psum[:, slot_bank(s), :], ACT.Copy).then_inc(pown_ready, 1)

            def square_centred(u, l):
                act.wait_ge(hc_ready, nth(u, LANES, l))
                nc.scalar.activation(hsq[l], hc[l], ACT.Square).then_inc(hsq_ready, 1)

            def root(u, l):
                act.wait_ge(var_kept, nth(u, LANES, l))
                nc.scalar.activation(std[l], var[l], ACT.Sqrt).then_inc(std_ready, 1)

            def gain_and_bias(u, l):
                act.wait_ge(hn_ready, nth(u, LANES, l))
                nc.scalar.activation(h2[l], hc[l], ACT.Identity, bias=lnb_sb[:, 0:1],
                                     scale=lng_sb[:, 0:1]).then_inc(hln_ready, 1)

            def gelu(u, l):
                for f, (f0, m) in enumerate(HID_TILES):
                    act.wait_ge(hidden_ready, nth(u, LANES * NF, l * NF + f))
                    nc.scalar.activation(ffn[l][0:m, f, :], psum[0:m, G_BANK[f], :], ACT.Gelu,
                                         bias=b1_sb[0:m, 1, f:f + 1]).then_inc(gelu_ready, 1)

            with act.Fori(0, DEPTH) as layer:
                wait_alone(act, w_in, nth(layer, LAYER_DMAS * 16, LAYER_DMAS * 16 - 1))
                with act.Fori(0, BATCH // LANES) as b:
                    u = layer * (BATCH // LANES) + b
                    square_and_values(u, 0)
                    keep_turned_qk(u, 0)
                    for g in range(TILES):
                        exponentials(u, 2 * g)
                        if g + 1 < TILES:
                            square_and_values(u, g + 1)
                        exponentials(u, 2 * g + 1)
                        keep_own(u, 2 * g)
                        if g + 1 < TILES:
                            keep_turned_qk(u, g + 1)
                        keep_own(u, 2 * g + 1)
                    square_centred(u, 0)
                    square_centred(u, 1)
                    root(u, 0)
                    root(u, 1)
                    gain_and_bias(u, 0)
                    gain_and_bias(u, 1)
                    gelu(u, 0)
                    gelu(u, 1)
            act.wait_ge(unit_done, BATCH + UNITS)
            by_chunk = res[:, :, :].rearrange("p b t -> p (b t)").rearrange("p (h c s) -> p c h s", h=2, s=CT)
            chunks = v_tok[:, 0].rearrange("p b t -> p (b t)").rearrange("p (c h s) -> p c h s", h=2, s=CT)
            nc.scalar.activation(chunks, by_chunk, ACT.Silu).then_inc(silu_ready, 1)
            for g in range(CHUNKS // 4):
                act.wait_ge(gate_turned, g + 1)
                nc.scalar.activation(gate[:, 4 * g:4 * g + 4, :].rearrange("p c n -> p (c n)"), psum[:, g, :],
                                     ACT.Copy).then_inc(gate_ready, 1)

        @block.vector
        def _(dve):
            dve.nop().then_inc(unit_done, BATCH)
            dve.wait_ge(tab_in, 16)
            dve.wait_ge(consts, 8)

            def shift_into(dst, src):
                nc.vector.tensor_copy(dst[0:HALF, :], src[0:HALF])
                nc.vector.memset(dst[HALF:P, 0:1], 0.0)
                return nc.vector.tensor_copy(dst[HALF:P, 1:SEQ], src[HALF:P, 0:SEQ - 1])

            def inverse_norms(u, g):
                dve.wait_ge(sq_ready, nth(u, TILES, g))
                nc.vector.reduce_sum(qk_stat[:, 0, :], qk_sq, AX_X).then_inc(ss_ready, 1)
                dve.wait_ge(ss_ready, nth(u, TILES, g))
                nc.vector.tensor_scalar(qk_stat[:, 2, :], qk_stat[:, 0, :], NORM_FLOOR_SQ, None, ALU.max) \
                    .then_inc(floor_ready, 1)
                dve.wait_ge(floor_ready, nth(u, TILES, g))
                rsqrt(nc, dve, qk_stat[:, 1, :], qk_stat[:, 2, :], qk_stat[:, 3, :], rsqrt_step,
                      (u * TILES + g) * RSQRT_STEPS)

            def normalise(u, g):
                nc.vector.tensor_tensor(qk_n, psum[:, 0:2, :].rearrange("p a (h d) -> p (a h) d", d=FD),
                                        qk_stat[:, 1, :].unsqueeze(2).broadcast_to([P, 2 * FH, FD]),
                                        ALU.mult).then_inc(qkn_ready, 1)
                dve.wait_ge(qkn_ready, nth(u, TILES, g))
                table = rot_gain[:, 0, :, g // LANES, :].unsqueeze(2).broadcast_to([P, 2, FH, FD])
                nc.vector.tensor_tensor(qk_cos.rearrange("p (a h) d -> p a h d", a=2),
                                        qk_n.rearrange("p (a h) d -> p a h d", a=2), table,
                                        ALU.mult).then_inc(cos_ready, 1)

            def add_sine_part(u, g):
                dve.wait_ge(cos_ready, nth(u, TILES, g))
                dve.wait_ge(sin_ready, nth(u, TILES, g))
                nc.vector.tensor_tensor(qk_rot, qk_cos, qk_sin, ALU.add).then_inc(rot_ready, 1)

            def mask_and_max(u, s):
                t = s // 2 // LANES
                dve.wait_ge(sim_ready, nth(u, STEPS, s))
                banks = psum[:, slot_bank(s):slot_bank(s) + 2, 0:2 * KEYS].rearrange("p a (h k) -> p a h k", k=KEYS)
                nc.vector.tensor_tensor(
                    s_mask[:, heads(s), :].rearrange("p (a h) k -> p a h k", h=2), banks,
                    mask[:, min(t, 1), :].unsqueeze(1).unsqueeze(1).broadcast_to([P, 2, 2, KEYS]),
                    ALU.add).then_inc(masked_ready, 1)
                dve.wait_ge(masked_ready, nth(u, STEPS, s))
                nc.vector.reduce_max(s_stat[:, 0, heads(s)], s_mask[:, heads(s), :], AX_X).then_inc(max_ready, 1)
                dve.wait_ge(max_ready, nth(u, STEPS, s))
                nc.vector.tensor_scalar(s_stat[:, 1, heads(s)], s_stat[:, 0, heads(s)], -QK_SCALE, None, ALU.mult) \
                    .then_inc(negmax_ready, 1)

            def inverse_sums(u, s):
                dve.wait_ge(exp_ready, nth(u, STEPS, s))
                nc.vector.reciprocal(s_stat[:, 3, heads(s)], s_stat[:, 2, heads(s)]).then_inc(rsum_ready, 1)

            def keep_prev(u, s):
                if s // 2 >= LANES:
                    dve.wait_ge(p_turned, nth(u, STEPS, s))
                    nc.vector.tensor_copy(p_prev[:, heads(s), :].rearrange("p h n -> p (h n)"),
                                          psum[:, slot_bank(s) + 1, :]).then_inc(pprev_ready, 1)

            def keep_outputs(u, s):
                g = s // 2
                lane, t = g % LANES, g // LANES
                dve.wait_ge(pv_ready, nth(u, STEPS, s))
                pairs = slice((s % 2) * HH // 2, (s % 2 + 1) * HH // 2)
                nc.vector.tensor_copy(o_t[lane][:, pairs, t * P:(t + 1) * P],
                                      psum[:, 7, :].rearrange("p (h n) -> p h n", n=P)[:, pairs]).then_inc(ot_ready, 1)

            def add_attention(u, l, x):
                dve.wait_ge(wo_ready, nth(u, LANES, l))
                nc.vector.tensor_tensor(x, x, psum[:, LANE_BANK[l], :], ALU.add).then_inc(res_mid, 1)
                wait_alone(dve, res_mid, nth(u, LANES, l))
                shift_into(h2[l], x).then_inc(h2_ready, 1)

            def centre(u, l):
                dve.wait_ge(mean_ready, nth(u, LANES, l))
                nc.vector.tensor_tensor(hc[l], h2[l], psum[:, LANE_BANK[l], :], ALU.subtract).then_inc(hc_ready, 1)

            def keep_variance(u, l):
                dve.wait_ge(var_ready, nth(u, LANES, l))
                nc.vector.tensor_scalar(var[l], psum[:, LANE_BANK[l], :], LN_EPS, None, ALU.add).then_inc(var_kept, 1)

            def divide_by_root(u, l):
                n = LANES * 3
                dve.wait_ge(std_ready, nth(u, LANES, l))
                nc.vector.reciprocal(rstd[l], std[l]).then_inc(refine, 1)
                dve.wait_ge(refine, nth(u, n, 3 * l))
                nc.vector.scalar_tensor_tensor(out=std[l], in0=rstd[l], scalar=-0.5, in1=rstd[l],
                                               op0=ALU.mult, op1=ALU.mult).then_inc(refine, 1)
                dve.wait_ge(refine, nth(u, n, 3 * l + 1))
                nc.vector.tensor_tensor(std[l], std[l], var[l], ALU.mult).then_inc(refine, 1)
                dve.wait_ge(refine, nth(u, n, 3 * l + 2))
                nc.vector.scalar_tensor_tensor(out=rstd[l], in0=std[l], scalar=1.5, in1=rstd[l],
                                               op0=ALU.add, op1=ALU.mult).then_inc(rstd_ready, 1)
                dve.wait_ge(rstd_ready, nth(u, LANES, l))
                nc.vector.tensor_tensor(hc[l], hc[l], rstd[l], ALU.mult).then_inc(hn_ready, 1)

            def apply_gate(u, l):
                for f, (f0, m) in enumerate(HID_TILES):
                    dve.wait_ge(gelu_ready, nth(u, LANES * NF, l * NF + f))
                    nc.vector.scalar_tensor_tensor(out=ffn[l][0:m, f, :], in0=psum[0:m, A_BANK[f], :],
                                                   scalar=b1_sb[0:m, 0, f:f + 1], in1=ffn[l][0:m, f, :],
                                                   op0=ALU.add, op1=ALU.mult).then_inc(ffn_ready, 1)

            def add_feed_forward(u, l, x):
                dve.wait_ge(w2_ready, nth(u, LANES, l))
                nc.vector.scalar_tensor_tensor(out=x, in0=psum[:, LANE_BANK[l], :], scalar=b2_sb[:, 0:1],
                                               in1=x, op0=ALU.add, op1=ALU.add).then_inc(unit_done, 1)

            with dve.Fori(0, DEPTH) as layer:
                dve.wait_ge(w_in, nth(layer, LAYER_DMAS * 16, LAYER_DMAS * 16 - 1))
                for n in range(2):
                    gain = qk_gain[:, n, :].unsqueeze(1)
                    nc.vector.tensor_tensor(rot_gain[:, 0, n], rot_sb[:, 0, n], gain.broadcast_to([P, QT, FD]), ALU.mult)
                    for half in range(2):
                        to = slice(half * 32, half * 32 + 32)
                        of = slice(32 - half * 32, 64 - half * 32)
                        last = nc.vector.tensor_tensor(rot_gain[:, 1, n, :, to], rot_sb[:, 1, n, :, to],
                                                       gain[:, :, of].broadcast_to([P, QT, 32]), ALU.mult)
                last.then_inc(gain_ready, 1)
                wait_alone(dve, gain_ready, layer + 1)
                with dve.Fori(0, BATCH // LANES) as b:
                    u = layer * (BATCH // LANES) + b
                    x = [res[:, b * LANES + l, :] for l in range(LANES)]
                    for l in range(LANES):
                        shift_into(h_t[:, l, :], x[l]).then_inc(h_ready, 1)
                    inverse_norms(u, 0)
                    normalise(u, 0)
                    add_sine_part(u, 0)
                    for g in range(TILES):
                        mask_and_max(u, 2 * g)
                        if g:
                            keep_outputs(u, 2 * g - 1)
                        if g + 1 < TILES:
                            inverse_norms(u, g + 1)
                        inverse_sums(u, 2 * g)
                        mask_and_max(u, 2 * g + 1)
                        if g + 1 < TILES:
                            normalise(u, g + 1)
                        keep_prev(u, 2 * g)
                        inverse_sums(u, 2 * g + 1)
                        if g + 1 < TILES:
                            add_sine_part(u, g + 1)
                        else:
                            add_attention(u, 0, x[0])
                        keep_outputs(u, 2 * g)
                        keep_prev(u, 2 * g + 1)
                    centre(u, 0)
                    keep_outputs(u, STEPS - 1)
                    keep_variance(u, 0)
                    add_attention(u, 1, x[1])
                    centre(u, 1)
                    divide_by_root(u, 0)
                    keep_variance(u, 1)
                    divide_by_root(u, 1)
                    apply_gate(u, 0)
                    apply_gate(u, 1)
                    add_feed_forward(u, 0, x[0])
                    add_feed_forward(u, 1, x[1])
                    wait_alone(dve, unit_done, nth(u, LANES, LANES - 1) + BATCH)
            dve.wait_ge(keep["lin_w_in"], 3 * 16)
            for n in range(3):
                nc.vector.tensor_reduce(largest[:, n:n + 1], raw_weights(keep, n), AX_X, ALU.max,
                                        apply_absolute_value=True).then_inc(largest_ready, 1)

        @block.tensor
        def _(pe):
            pe.wait_ge(consts, 8)

            def project(u, g):
                lane, t = g % LANES, g // LANES
                if g < LANES:
                    pe.wait_ge(h_ready, nth(u, LANES, lane))
                if g:
                    pe.wait_ge(v_ready, nth(u, TILES, g - 1))
                    pe.wait_ge(qkt_ready, nth(u, TILES, g - 1))
                for n in range(3):
                    last = nc.tensor.matmul(psum[:, n, :], h_t[:, lane, t * P:(t + 1) * P],
                                            wqkv_sb[:, n * INNER:(n + 1) * INNER], start=True, stop=True)
                last.then_inc(qkv_ready, 1)

            def turn_qk(u, g):
                pe.wait_ge(rot_ready, nth(u, TILES, g))
                for n in range(2):
                    for pair in range(FH // 2):
                        pairs = qk_rot[:, n * FH + 2 * pair:n * FH + 2 * pair + 2, :]
                        last = nc.tensor.transpose(psum[:, n, pair * P:(pair + 1) * P],
                                                   pairs.rearrange("p h d -> p (h d)"), ident[:, :])
                last.then_inc(qk_turned, 1)

            def copies_kept(u, s):
                pe.wait_ge(pown_ready, nth(u, STEPS, s))
                if s // 2 >= LANES:
                    pe.wait_ge(pprev_ready, nth(u, STEPS - 2 * LANES, s - 2 * LANES))

            def scores(u, s):
                g = s // 2
                lane, t = g % LANES, g // LANES
                pe.wait_ge(qkt_ready, nth(u, TILES, g))
                if s >= 2:
                    copies_kept(u, s - 2)
                for n in range(HH):
                    h = (s % 2) * HH + n
                    last = nc.tensor.matmul(psum[:, slot_bank(s) + n // 2, (n % 2) * KEYS:(n % 2 + 1) * KEYS],
                                            q_t[:, h, :], k_t[:, lane, h // 2, t * P:t * P + KEYS],
                                            start=True, stop=True)
                last.then_inc(sim_ready, 1)

            def turn_probabilities(u, s):
                pe.wait_ge(prob_ready, nth(u, STEPS, s))
                for n in range(HH):
                    h = (s % 2) * HH + n
                    last = nc.tensor.transpose(psum[:, slot_bank(s), n * P:(n + 1) * P], prob[:, h, P:2 * P], ident[:, :])
                    if s // 2 >= LANES:
                        last = nc.tensor.transpose(psum[:, slot_bank(s) + 1, n * P:(n + 1) * P], prob[:, h, 0:P],
                                                   ident[:, :])
                last.then_inc(p_turned, 1)

            def times_values(u, s):
                g = s // 2
                lane, t = g % LANES, g // LANES
                copies_kept(u, s)
                if s:
                    pe.wait_ge(ot_ready, nth(u, STEPS, s - 1))
                for n in range(HH):
                    h = (s % 2) * HH + n
                    o = psum[(h % 2) * HALF:(h % 2 + 1) * HALF, 7, (h // 2) * P:(h // 2 + 1) * P]
                    last = nc.tensor.matmul(o, v_tok[:, lane, t, h * FD:(h + 1) * FD], p_own[:, h, :],
                                            start=True, stop=(t == 0))
                    if t:
                        last = nc.tensor.matmul(o, v_tok[:, lane, t - 1, h * FD:(h + 1) * FD], p_prev[:, h, :],
                                                start=False, stop=True)
                last.then_inc(pv_ready, 1)

            def project_attention(u, l):
                pe.wait_ge(ot_ready, nth(u, STEPS, 2 * (TILES - LANES + l) + 1))
                for pair in range(FH // 2):
                    last = nc.tensor.matmul(psum[:, LANE_BANK[l], :], fwo_sb[:, pair, :], o_t[l][:, pair, :],
                                            start=(pair == 0), stop=(pair == FH // 2 - 1))
                last.then_inc(wo_ready, 1)

            def average(of, ready, done, l):
                pe.wait_ge(*ready)
                nc.tensor.matmul(psum[:, LANE_BANK[l], :], mean_w[:, :], of[l], start=True, stop=True).then_inc(done, 1)

            def hidden(u, l):
                pe.wait_ge(hln_ready, nth(u, LANES, l))
                for f, (f0, m) in enumerate(HID_TILES):
                    if l:
                        pe.wait_ge(ffn_ready, nth(u, LANES * NF, (l - 1) * NF + f))
                    nc.tensor.matmul(psum[0:m, G_BANK[f], :], w1_sb[:, HID + f0:HID + f0 + m], h2[l],
                                     start=True, stop=True)
                    nc.tensor.matmul(psum[0:m, A_BANK[f], :], w1_sb[:, f0:f0 + m], h2[l],
                                     start=True, stop=True).then_inc(hidden_ready, 1)

            def project_hidden(u, l):
                for f, (f0, m) in enumerate(HID_TILES):
                    pe.wait_ge(ffn_ready, nth(u, LANES * NF, l * NF + f))
                    last = nc.tensor.matmul(psum[:, LANE_BANK[l], :], w2_sb[0:m, f, :], ffn[l][0:m, f, :],
                                            start=(f == 0), stop=(f == NF - 1))
                last.then_inc(w2_ready, 1)

            with pe.Fori(0, DEPTH) as layer:
                wait_alone(pe, w_in, nth(layer, LAYER_DMAS * 16, LAYER_DMAS * 16 - 1))
                with pe.Fori(0, BATCH // LANES) as b:
                    u = layer * (BATCH // LANES) + b
                    project(u, 0)
                    turn_qk(u, 0)
                    for g in range(TILES):
                        scores(u, 2 * g)
                        if g + 1 < TILES:
                            project(u, g + 1)
                        if g:
                            times_values(u, 2 * g - 1)
                        scores(u, 2 * g + 1)
                        if g + 1 == TILES:
                            project_attention(u, 0)
                        turn_probabilities(u, 2 * g)
                        times_values(u, 2 * g)
                        if g + 1 < TILES:
                            turn_qk(u, g + 1)
                        else:
                            average(h2, (h2_ready, nth(u, LANES, 0)), mean_ready, 0)
                        turn_probabilities(u, 2 * g + 1)
                    times_values(u, STEPS - 1)
                    average(hsq, (hsq_ready, nth(u, LANES, 0)), var_ready, 0)
                    project_attention(u, 1)
                    average(h2, (h2_ready, nth(u, LANES, 1)), mean_ready, 1)
                    average(hsq, (hsq_ready, nth(u, LANES, 1)), var_ready, 1)
                    hidden(u, 0)
                    hidden(u, 1)
                    project_hidden(u, 0)
                    project_hidden(u, 1)
            pe.wait_ge(silu_ready, 1)
            chunks = v_tok[:, 0].rearrange("p b (c n) -> p (b c) n", n=P)
            for c in range(CHUNKS):
                last = nc.tensor.transpose(psum[:, c // 4, (c % 4) * P:(c % 4 + 1) * P], chunks[:, c, :], ident[:, :])
                if c % 4 == 3:
                    last.then_inc(gate_turned, 1)


def raw_weights(keep, n):
    return keep["work"][:, n * LH * LD:(n + 1) * LH * LD]


def split_weights(nc, keep):
    peak, w_parts, scale = keep["peak"], keep["w_parts"], keep["scale"]
    with ExitStack() as ctx:
        def sem(name):
            return ctx.enter_context(nc.semaphore(name))

        scale_step, scale_ready, high_ready, low_ready = (sem("scale_step"), sem("scale_ready"),
                                                          sem("w_high_ready"), sem("w_low_ready"))
        block = ctx.enter_context(nc.Block())

        @block.vector
        def _(dve):
            steps = [
                lambda: nc.vector.tensor_scalar(scale[:, :, 1], peak[:, 0:3], 2.0 ** -60, None, ALU.max),
                lambda: nc.vector.tensor_scalar(scale[:, :, 2].bitcast(I32), scale[:, :, 1].bitcast(I32),
                                                0x7F800000, None, ALU.bitwise_and),
                lambda: nc.vector.tensor_scalar(scale[:, :, 3], scale[:, :, 2], 2.0 ** (1 - W_TOP), None, ALU.mult),
                lambda: nc.vector.reciprocal(scale[:, :, 0], scale[:, :, 3])]
            for k, step in enumerate(steps):
                step().then_inc(scale_step, 1)
                dve.wait_ge(scale_step, k + 1)
            dve.nop().then_inc(scale_ready, 1)
            nc.vector.tensor_tensor(scale[:, 0, 1:2], scale[:, 0, 0:1], scale[:, 1, 0:1], ALU.mult) \
                .then_inc(scale_step, 1)
            dve.wait_ge(scale_step, 5)
            nc.vector.tensor_scalar(scale[:, 0, 2:3], scale[:, 0, 1:2], LEPS / LSCALE * K_SHIFT, None, ALU.mult)
            for k, n in enumerate((1, 2, 0)):
                dve.wait_ge(high_ready, k + 1)
                nc.vector.scalar_tensor_tensor(out=w_parts[:, n, 1, :], in0=raw_weights(keep, n),
                                               scalar=scale[:, n, 0:1], in1=w_parts[:, n, 0, :],
                                               op0=ALU.mult, op1=ALU.subtract)

        @block.scalar
        def _(act):
            act.wait_ge(scale_ready, 1)
            for n in (1, 2, 0):
                nc.scalar.activation(w_parts[:, n, 0, :], raw_weights(keep, n), ACT.Identity,
                                     scale=scale[:, n, 0:1]).then_inc(high_ready, 1)


def linear_branch(nc, keep, wo, bo, out):
    x_tok, xn_parts, gate, psum = (keep[n] for n in ("x_tok", "xn_parts", "gate", "psum"))
    w_parts, scale, work = keep["w_parts"], keep["scale"], keep["work"]
    PAIRS = LH // 2
    GROUP = 8
    NG = PAIRS // GROUP
    NT = CT // GROUP
    SLOTS = 3
    HIGH, LOW = 0, 1
    PASSES = [(HIGH, HIGH), (HIGH, LOW), (LOW, HIGH)]
    OUT_V = [use for g in range(NG) for use in (("out", 2 * g), ("out", 2 * g + 1), ("v", g))]
    USES = [("sum", 0)] + [("q", g) for g in range(NG)] + [("k", g) for g in range(NG)] + OUT_V
    assert len(USES) % SLOTS == 0
    PER = {"k": NG, "v": NG, "sum": 1, "q": NG, "out": NT}

    with ExitStack() as ctx:
        def sb(name, shape, dtype=FP32):
            return ctx.enter_context(nc.sbuf_tensor(name, shape, dtype))

        def sem(name):
            return ctx.enter_context(nc.semaphore(name))

        q_f = work[:, 0:CT * LH].rearrange("p (s i) -> p s i", i=LH)
        v_f = work[:, CT * LH:CT * (2 * LH + 2)].rearrange("p (s j) -> p s j", j=LH + 2)
        o_s = work[:, CT * (2 * LH + 2):WORK].rearrange("p (j t) -> p j t", t=P)
        wo_sb = sb("wo_sb", [P, PAIRS, DIM])
        bo_sb = sb("bo_sb", [P, DIM])
        pair_sum = sb("pair_sum", [P, 2, HALF])
        x_kv = sb("x_kv", [P, 2, 2, CT], FP16)
        x_q = sb("x_q", [P, 2, 2, CT], FP16)
        k_acc = sb("k_acc", [P, GROUP, P])
        k_heads = sb("k_heads", [P, P])
        k_sum = sb("k_sum", [P, CT])
        q_parts = sb("q_parts", [P, 2, CT, 2, LH], FP16)
        v_parts = sb("v_parts", [P, 2, CT, LH + 2], FP16)
        denom = sb("denom", [P, 2, 2, GROUP])
        y_sb = sb("y_sb", [P, DIM])
        y_step = sb("y_step", [P, 2, DIM])

        wo_in, consts = sem("lin_wo_in"), sem("lin_consts")
        xkv_ready, xq_ready = sem("xkv_ready"), sem("xq_ready")
        filled = {kind: sem(f"{kind}_filled") for kind in PER}
        read = {kind: sem(f"{kind}_read") for kind in PER}
        k_heads_ready = sem("k_heads_ready")
        q_scaled, q_high, q_low_a, q_low_b, v_high, v_low = (
            sem("q_scaled"), sem("q_high"), sem("q_low_a"), sem("q_low_b"), sem("v_high"), sem("v_low"))
        wo_scaled = sem("wo_scaled")
        denom_ready, recip_ready = sem("denom_ready"), sem("recip_ready")
        y_filled, y_ready, y_used, y_chain = sem("y_filled"), sem("y_ready"), sem("y_used"), sem("y_chain")
        o_ready, stored = sem("o_ready"), sem("stored")
        block = ctx.enter_context(nc.Block())

        def slot(kind, g):
            first = 2 * (USES.index((kind, g)) % SLOTS)
            return psum[:, first:first + 2, :].rearrange("p a (n c) -> p (a n) c", c=P)

        def heads_of(buffer, g):
            return buffer.rearrange("p s (a n) -> p s a n", a=2)[:, :, :, g * GROUP:(g + 1) * GROUP]

        def low_q_operands(g, half):
            rows = slice(half * HALF, (half + 1) * HALF)
            return (heads_of(q_parts[rows, LOW, :, half, :], g), heads_of(q_f[rows], g),
                    heads_of(q_parts[rows, HIGH, :, half, :], g))

        @block.sync
        def _(sp):
            rows = wo.rearrange("(ia ib ja jb) n -> jb ib ia ja n", ia=LH // 2, ib=2, ja=LH // 2, jb=2)
            for jb in range(2):
                for ib in range(2):
                    p0 = jb * HALF + ib * 32
                    sp.dma_start(wo_sb[p0:p0 + 32, :, :], rows[jb, ib]).then_inc(wo_in, 16)
            sp.dma_start(bo_sb[:, :], bo.partition_broadcast(P)).then_inc(wo_in, 16)
            out_by_chunk = out.rearrange("b t d -> (b t) d").rearrange("(h c s) d -> h c s d", h=2, s=CT)
            with sp.Fori(0, CHUNKS) as c:
                sp.wait_ge(o_ready, c + 1)
                for h in range(2):
                    sp.dma_start(out_by_chunk[h, c], x_tok[h * HALF:(h + 1) * HALF, c, :]).then_inc(stored, 16)
            sp.wait_ge(stored, CHUNKS * 2 * 16)

        @block.gpsimd
        def _(pool):
            by_chunk = xn_parts[:, :, :].rearrange("p a (h c s) -> p a c h s", h=2, s=CT)

            def take_tokens(dst, c, ready):
                for part in (HIGH, LOW):
                    last = nc.gpsimd.tensor_copy(dst[:, part], by_chunk[:, part, c])
                last.then_inc(ready, 1)

            take_tokens(x_kv, 0, xkv_ready)
            take_tokens(x_q, 0, xq_ready)
            nc.gpsimd.memset(pair_sum[:, :, :], 0.0).then_inc(consts, 1)
            nc.gpsimd.memset(v_parts[:, HIGH, :, LH:LH + 1], 1.0).then_inc(consts, 1)
            nc.gpsimd.memset(v_parts[:, LOW, :, LH:LH + 1], 0.0).then_inc(consts, 1)
            pool.wait_ge(consts, 3)
            for k, base in enumerate((0, -HALF)):
                nc.gpsimd.affine_select(out=pair_sum[:, :, :], in_=pair_sum[:, :, :], compare_op=ALU.not_equal,
                                        fill=1.0, base=base, pattern=[[0, 2], [-1, HALF]],
                                        channel_multiplier=1).then_inc(consts, 1)
                pool.wait_ge(consts, 4 + k)
            for half in range(2):
                for part in (HIGH, LOW):
                    zeros = q_parts[half * HALF:(half + 1) * HALF, part, :, 1 - half, :]
                    nc.gpsimd.memset(zeros, 0.0).then_inc(consts, 1)
                pool.wait_ge(consts, 3 + 2 + 2 * (half + 1))
            pool.nop().then_inc(y_used, 1)

            def low_of_v(c):
                for g in range(NG):
                    pool.wait_ge(v_high, nth(c, NG, g))
                    nc.gpsimd.tensor_tensor(heads_of(v_parts[:, LOW, :, 0:LH], g), heads_of(v_f[:, :, 0:LH], g),
                                            heads_of(v_parts[:, HIGH, :, 0:LH], g), ALU.subtract).then_inc(v_low, 1)

            def low_of_q(c):
                for g in range(NG):
                    wait_alone(pool, q_high, nth(c, 2 * NG, 2 * g + 1))
                    nc.gpsimd.tensor_tensor(*low_q_operands(g, 1), ALU.subtract).then_inc(q_low_b, 1)
                    wait_alone(pool, q_low_b, nth(c, NG, g))

            def finish(c):
                pool.wait_ge(y_ready, c + 1)
                nc.gpsimd.tensor_tensor(y_step[:, 0, :], y_sb[:, :], bo_sb[:, :], ALU.add).then_inc(y_chain, 1)
                pool.wait_ge(y_chain, nth(c, 2))
                pool.nop().then_inc(y_used, 1)
                nc.gpsimd.tensor_tensor(y_step[:, 1, :], y_step[:, 0, :], gate[:, c, :], ALU.mult).then_inc(y_chain, 1)
                pool.wait_ge(y_chain, nth(c, 2, 1))
                nc.gpsimd.tensor_tensor(x_tok[:, c, :], y_step[:, 1, :], x_tok[:, c, :], ALU.add).then_inc(o_ready, 1)

            low_of_v(0)
            pool.wait_ge(wo_in, 5 * 16)

            def turn(c, first, last):
                if not last:
                    wait_alone(pool, filled["v"], nth(c, NG, NG - 1))
                    take_tokens(x_kv, c + 1, xkv_ready)
                    wait_alone(pool, xkv_ready, c + 2)
                else:
                    pool.wait_ge(v_low, nth(c, NG, NG - 1))
                low_of_q(c)
                if not last:
                    take_tokens(x_q, c + 1, xq_ready)
                if not first:
                    finish(c - 1)
                if not last:
                    low_of_v(c + 1)

            turn(0, True, False)
            with pool.Fori(1, CHUNKS - 1) as c:
                turn(c, False, False)
            turn(CHUNKS - 1, False, True)
            finish(CHUNKS - 1)

        @block.scalar
        def _(act):
            def take_v(c, outs_filled):
                for g in range(NG):
                    act.wait_ge(filled["v"], nth(c, NG, g))
                    for half in range(2):
                        for par in range(2):
                            src = slot("v", g)[par * HALF:(par + 1) * HALF, :, half * CT:(half + 1) * CT]
                            j0 = par * PAIRS + g * GROUP
                            dst = v_f[half * HALF:(half + 1) * HALF, :, j0:j0 + GROUP].rearrange("p s j -> p j s")
                            last = nc.scalar.activation(dst, src, ACT.Copy)
                    last.then_inc(read["v"], 1)
                if outs_filled is not None:
                    act.wait_ge(filled["out"], outs_filled)
                for g in range(NG):
                    act.wait_ge(read["v"], nth(c, NG, g))
                    nc.scalar.activation(heads_of(v_parts[:, HIGH, :, 0:LH], g), heads_of(v_f[:, :, 0:LH], g),
                                         ACT.Copy).then_inc(v_high, 1)

            def take_q(c):
                for g in range(NG):
                    act.wait_ge(filled["q"], nth(c, NG, g))
                    for half in range(2):
                        for par in range(2):
                            src = slot("q", g)[par * HALF:(par + 1) * HALF, :, half * CT:(half + 1) * CT]
                            i0 = par * PAIRS + g * GROUP
                            dst = q_f[half * HALF:(half + 1) * HALF, :, i0:i0 + GROUP].rearrange("p s i -> p i s")
                            last = nc.scalar.activation(dst, src, ACT.Relu)
                    last.then_inc(read["q"], 1)
                for g in range(NG):
                    act.wait_ge(q_scaled, nth(c, NG, g))
                    for half in range(2):
                        rows = slice(half * HALF, (half + 1) * HALF)
                        nc.scalar.activation(heads_of(q_parts[rows, HIGH, :, half, :], g), heads_of(q_f[rows], g),
                                             ACT.Copy).then_inc(q_high, 1)

            def take_y(c):
                act.wait_ge(y_filled, c + 1)
                act.wait_ge(y_used, c + 1)
                nc.scalar.activation(y_sb[:, :], psum[:, 6, 0:DIM], ACT.Copy).then_inc(y_ready, 1)

            take_v(0, None)
            take_q(0)
            take_v(1, nth(0, NT, NT - 1))
            with act.Fori(1, CHUNKS - 1) as c:
                take_q(c)
                take_y(c - 1)
                take_v(c + 1, nth(c, NT, NT - 1))
            take_q(CHUNKS - 1)
            take_y(CHUNKS - 2)
            take_y(CHUNKS - 1)

        @block.vector
        def _(dve):
            dve.wait_ge(wo_in, 5 * 16)
            nc.vector.tensor_scalar(wo_sb[:, :, :], wo_sb[:, :, :], scale[:, 2, 3:4], None, ALU.mult) \
                .then_inc(wo_scaled, 1)

            def sum_k(c):
                for g in range(NG):
                    dve.wait_ge(filled["k"], nth(c, NG, g))
                    if g == 0:
                        nc.vector.tensor_scalar(k_acc[:, :, :], slot("k", g), 0.0, None, ALU.max).then_inc(read["k"], 1)
                    else:
                        dve.wait_ge(read["k"], nth(c, NG, g - 1))
                        nc.vector.scalar_tensor_tensor(out=k_acc[:, :, :], in0=slot("k", g), scalar=0.0,
                                                       in1=k_acc[:, :, :], op0=ALU.max, op1=ALU.add) \
                            .then_inc(read["k"], 1)
                dve.wait_ge(read["k"], nth(c, NG, NG - 1))
                nc.vector.reduce_sum(k_heads[:, :], k_acc[:, :, :].rearrange("p n t -> p t n"), AX_X) \
                    .then_inc(k_heads_ready, 1)

            def scale_q(c):
                dve.wait_ge(filled["sum"], c + 1)
                for half in range(2):
                    rows = slice(half * HALF, (half + 1) * HALF)
                    last = nc.vector.tensor_scalar(k_sum[rows, :], slot("sum", 0)[rows, 0, half * CT:(half + 1) * CT],
                                                   K_SHIFT, None, ALU.mult)
                last.then_inc(read["sum"], 1)
                dve.wait_ge(read["sum"], c + 1)
                for g in range(NG):
                    dve.wait_ge(read["q"], nth(c, NG, g))
                    of_group = heads_of(q_f, g)
                    nc.vector.tensor_tensor(of_group, of_group, k_sum[:, :].unsqueeze(2).unsqueeze(3)
                                            .broadcast_to([P, CT, 2, GROUP]), ALU.mult).then_inc(q_scaled, 1)
                for g in range(NG):
                    dve.wait_ge(q_high, nth(c, 2 * NG, 2 * g))
                    nc.vector.tensor_tensor(*low_q_operands(g, 0), ALU.subtract).then_inc(q_low_a, 1)

            def add_eps(c, g):
                dve.wait_ge(filled["out"], nth(c, NT, g))
                nc.vector.tensor_scalar(denom[:, g % 2, 0, :], slot("out", g)[:, :, LH], scale[:, 0, 2:3], None,
                                        ALU.add).then_inc(denom_ready, 1)

            def take_out(c):
                add_eps(c, 0)
                for g in range(NT):
                    dve.wait_ge(denom_ready, nth(c, NT, g))
                    nc.vector.reciprocal(denom[:, g % 2, 1, :], denom[:, g % 2, 0, :]).then_inc(recip_ready, 1)
                    if g + 1 < NT:
                        add_eps(c, g + 1)
                    dve.wait_ge(recip_ready, nth(c, NT, g))
                    for half in range(2):
                        for par in range(2):
                            rows = slice(half * HALF, (half + 1) * HALF)
                            s0 = half * CT + g * GROUP
                            dst = o_s[par * HALF:(par + 1) * HALF, :, s0:s0 + GROUP].rearrange("p j s -> p s j")
                            last = nc.vector.tensor_tensor(
                                dst, slot("out", g)[rows, :, par * PAIRS:(par + 1) * PAIRS],
                                denom[rows, g % 2, 1, :].unsqueeze(2).broadcast_to([HALF, GROUP, PAIRS]), ALU.mult)
                    last.then_inc(read["out"], 1)

            sum_k(0)
            with dve.Fori(0, CHUNKS - 1) as c:
                scale_q(c)
                sum_k(c + 1)
                take_out(c)
            scale_q(CHUNKS - 1)
            take_out(CHUNKS - 1)

        @block.tensor
        def _(pe):
            weights = {"q": 0, "k": 1, "v": 2}
            tokens = {"q": x_q, "k": x_kv, "v": x_kv}

            def slot_free(kind, g, c):
                n = USES.index((kind, g))
                before, i = USES[n - SLOTS]
                of_chunk = c + (before in ("k", "v")) - (n < SLOTS)
                pe.wait_ge(read[before], nth(of_chunk, PER[before], i))

            def project_group(kind, g):
                for n in range(GROUP):
                    cols = slice((g * GROUP + n) * P, (g * GROUP + n + 1) * P)
                    for k, (a, b) in enumerate(PASSES):
                        last = nc.tensor.matmul(slot(kind, g)[:, n, :], w_parts[:, weights[kind], a, cols],
                                                tokens[kind][:, b].rearrange("p h s -> p (h s)"),
                                                start=(k == 0), stop=(k == len(PASSES) - 1))
                last.then_inc(filled[kind], 1)

            def out_group(g):
                for n in range(GROUP):
                    for k, (a, b) in enumerate(PASSES):
                        last = nc.tensor.matmul(slot("out", g)[:, n, 0:LH + 1],
                                                q_parts[:, a, g * GROUP + n].rearrange("p h i -> p (h i)"),
                                                v_parts[:, b, g * GROUP + n, 0:LH + 1],
                                                start=(k == 0), stop=(k == len(PASSES) - 1))
                last.then_inc(filled["out"], 1)

            def project_out(c):
                pe.wait_ge(read["out"], nth(c, NT, NT - 1))
                for n in range(PAIRS):
                    last = nc.tensor.matmul(psum[:, 6, 0:DIM], o_s[:, n, :], wo_sb[:, n, :],
                                            start=(n == 0), stop=(n == PAIRS - 1))
                last.then_inc(y_filled, 1)

            def turn(c, first, last):
                if not first:
                    slot_free("sum", 0, c)
                pe.wait_ge(k_heads_ready, c + 1)
                nc.tensor.matmul(slot("sum", 0)[:, 0, :], pair_sum[:, :, :].rearrange("p a d -> p (a d)"),
                                 k_heads[:, :], start=True, stop=True).then_inc(filled["sum"], 1)
                pe.wait_ge(xq_ready, c + 1)
                for g in range(NG):
                    if not (first and g == 0):
                        slot_free("q", g, c)
                    project_group("q", g)
                if not first:
                    project_out(c - 1)
                if not last:
                    pe.wait_ge(xkv_ready, c + 2)
                    for g in range(NG):
                        slot_free("k", g, c)
                        project_group("k", g)
                pe.wait_ge(q_low_a, nth(c, NG, NG - 1))
                pe.wait_ge(q_low_b, nth(c, NG, NG - 1))
                pe.wait_ge(v_low, nth(c, NG, NG - 1))
                for kind, g in OUT_V:
                    if kind == "out":
                        if not last or g >= 2:
                            slot_free("out", g, c)
                        out_group(g)
                    elif not last:
                        slot_free("v", g, c)
                        project_group("v", g)

            pe.wait_ge(xkv_ready, 1)
            pe.wait_ge(consts, 3 + 2 + 4)
            pe.wait_ge(wo_scaled, 1)
            for g in range(NG):
                if g == SLOTS:
                    pe.wait_ge(read["k"], 1)
                project_group("k", g)
            for g in range(NG):
                pe.wait_ge(*((read["k"], NG) if g == 0 else (read["v"], g)))
                project_group("v", g)
            turn(0, True, False)
            with pe.Fori(1, CHUNKS - 1) as c:
                turn(c, False, False)
            turn(CHUNKS - 1, False, True)
            pe.wait_ge(y_ready, CHUNKS - 1)
            project_out(CHUNKS - 1)


def rotary_tables():
    import numpy as np
    f32 = np.float32
    half = np.arange(0, FD, 2, dtype=f32)
    inv_freq = (f32(1.0) / np.power(f32(10000.0), half / f32(FD), dtype=f32)).astype(f32)
    t = np.arange(SEQ, dtype=f32)
    freqs = t[:, None] * inv_freq[None, :]
    freqs = np.concatenate([freqs, freqs], axis=-1)
    base = (half + f32(0.4 * FD)) / f32(1.4 * FD)
    power = (t - SEQ // 2) / f32(WIN // 2)
    scale = np.power(base[None, :], power[:, None], dtype=f32)
    scale = np.concatenate([scale, scale], axis=-1)
    sign = np.where(np.arange(FD) < FD // 2, -1.0, 1.0).astype(f32)
    cos, sin = np.cos(freqs).astype(f32), np.sin(freqs).astype(f32) * sign
    tables = np.stack([np.stack([cos * scale, cos / scale]), np.stack([sin * scale, sin / scale])])
    tables = tables.reshape(2, 2, QT, P, FD).transpose(3, 0, 1, 2, 4)
    return np.ascontiguousarray(tables.reshape(P, -1).astype(f32))


_INS = ["L0_attn_x", "L0_attn_Wq", "L0_attn_Wk", "L0_attn_Wv", "L0_attn_Wo", "L0_attn_bo",
        "L0_ffn_wqkv", "L0_ffn_q_scale", "L0_ffn_k_scale", "L0_ffn_wo", "L0_ffn_ln_g", "L0_ffn_ln_b",
        "L0_ffn_w1", "L0_ffn_b1", "L0_ffn_w2", "L0_ffn_b2"]


def kernel(**inputs):
    import numpy as _np
    import concourse.bacc as _bacc
    from concourse import mybir as _mybir
    from concourse.bass_utils import run_bass_kernel_spmd as _run

    nc = _bacc.Bacc("TRN2", target_bir_lowering=False, num_devices=1)
    arrays, args = {}, []
    for name in _INS:
        a = _np.ascontiguousarray(inputs[name])
        arrays[f"in_{name}"] = a
        args.append(nc.dram_tensor(f"in_{name}", a.shape, _mybir.dt.from_np(a.dtype), kind="ExternalInput").ap())
    tables = rotary_tables()
    arrays["rotary"] = tables
    args.append(nc.dram_tensor("rotary", tables.shape, _mybir.dt.float32, kind="ExternalInput").ap())
    args.append(nc.dram_tensor("out_0", (BATCH, SEQ, DIM), _mybir.dt.float32, kind="ExternalOutput").ap())
    build(nc, *args)
    r = _run(nc, [arrays], core_ids=[0])
    return r.results[0]["out_0"]
```

```python
import concourse.bass as bass
from concourse import mybir
from contextlib import ExitStack

FP32 = mybir.dt.float32
FP16 = mybir.dt.float16
I32 = mybir.dt.int32
ALU = mybir.AluOpType
ACT = mybir.ActivationFunctionType
AX_X = mybir.AxisListType.X
REDUCE_MAX = bass.bass_isa.ReduceOp.max

BATCH, SEQ, DIM = 4, 512, 128
TOKENS = BATCH * SEQ
P = 128
LH, LD = 64, 64
LSCALE = LD ** -0.5
LEPS = 1e-6
DEPTH, FH, FD, WIN = 2, 8, 64, 64
INNER = FH * FD
HID = int(DIM * 4 * 2 / 3)
QK_SCALE = 8.0
LN_EPS = 1e-5
NORM_FLOOR_SQ = 1e-24
MASKED = -1e30
RSQRT_GUESS = 0x5F3759DF + 1
CT = 64
CHUNKS = TOKENS // (2 * CT)
HALF = P // 2
QT = SEQ // P
UNITS = DEPTH * BATCH
HID_TILES = [(f * P, min(P, HID - f * P)) for f in range(-(-HID // P))]
W_TOP = 8
K_SHIFT = 2.0 ** -(W_TOP + 7 + 6)
PARTS = 2
ST = CT // PARTS
NSTEPS = CHUNKS * PARTS
WORK = max(2 * LH * ST + 2 * LH * CT, 3 * LH * LD)
LANES = 2
KEYS = WIN + P


def nth(i, per_turn, k=0):
    return i * per_turn + k + 1


def wait_alone(engine, semaphore, value):
    engine.wait_ge(semaphore, value)
    engine.nop(nofuse=True)


RSQRT_STEPS = 11


def rsqrt(nc, dve, y, x, work, stepped, before):
    steps = [lambda: nc.vector.tensor_scalar(work.bitcast(I32), x.bitcast(I32), 1, -1,
                                             ALU.logical_shift_right, ALU.bitwise_xor),
             lambda: nc.vector.tensor_scalar(y.bitcast(I32), work.bitcast(I32), RSQRT_GUESS, None, ALU.add)]
    for _ in range(3):
        steps += [lambda: nc.vector.scalar_tensor_tensor(out=work, in0=y, scalar=-0.5, in1=y,
                                                         op0=ALU.mult, op1=ALU.mult),
                  lambda: nc.vector.tensor_tensor(work, work, x, ALU.mult),
                  lambda: nc.vector.scalar_tensor_tensor(out=y, in0=work, scalar=1.5, in1=y,
                                                         op0=ALU.add, op1=ALU.mult)]
    for k, step in enumerate(steps):
        step().then_inc(stepped, 1)
        dve.wait_ge(stepped, before + k + 1)


def build(nc, x, wq, wk, wv, wo, bo, wqkv, q_scale, k_scale, fwo, ln_g, ln_b,
          w1, b1, w2, b2, rot, out):
    with ExitStack() as ctx:
        def sb(name, shape, dtype=FP32, scope=ctx):
            return scope.enter_context(nc.sbuf_tensor(name, shape, dtype))

        keep = {
            "x_tok": sb("x_tok", [P, CHUNKS, DIM]),
            "xn_parts": sb("xn_parts", [P, 2, TOKENS], FP16),
            "gate": sb("gate", [P, CHUNKS, DIM]),
            "ident": sb("ident", [P, P]),
            "peak": sb("peak", [P, 4]),
            "work": sb("work", [P, WORK]),
            "psum": ctx.enter_context(nc.psum_tensor("psum", [P, 8, 512], FP32)),
            "lin_w_in": ctx.enter_context(nc.semaphore("lin_w_in")),
        }
        with ExitStack() as scope:
            keep["res"] = sb("res", [P, BATCH, SEQ], FP32, scope)
            weights = GateWeights(nc, scope, wqkv, q_scale, k_scale, fwo, ln_g, ln_b, w1, b1, w2, b2, rot)
            normalise_input(nc, keep, x, weights)
            gate_branch(nc, keep, weights, (wq, wk, wv))
        linear_branch(nc, keep, wo, bo, out)


class GateWeights:

    W_DMAS = 2 + len(HID_TILES)
    VEC_DMAS = DEPTH * (2 + 3 + 2 * len(HID_TILES))
    VECS = 3 + 2 * len(HID_TILES)

    def __init__(self, nc, scope, wqkv, q_scale, k_scale, fwo, ln_g, ln_b, w1, b1, w2, b2, rot):
        def sb(name, shape):
            return scope.enter_context(nc.sbuf_tensor(name, shape, FP32))

        def sem(name):
            return scope.enter_context(nc.semaphore(name))

        self.dram = (wqkv, q_scale, k_scale, fwo, ln_g, ln_b, w1, b1, w2, b2, rot)
        self.wqkv = sb("wqkv_sb", [P, 3 * INNER])
        self.fwo = sb("fwo_sb", [P, INNER // P, DIM])
        self.w1 = sb("w1_sb", [P, 2 * HID])
        self.w2 = sb("w2_sb", [P, len(HID_TILES), DIM])
        self.qk_gain = sb("qk_gain", [P, DEPTH, 2, FD])
        self.vec = sb("vec_all", [P, DEPTH, self.VECS])
        self.rot = sb("rot_sb", [P, 2, 2, QT, FD])
        self.vec_zero = sem("vec_zero")
        self.tab_in, self.vec_in, self.wqkv_in, self.w_in = sem("tab_in"), sem("vec_in"), sem("wqkv_in"), sem("w_in")

    def load_layer(self, sp, layer, wait_for):
        wqkv, _, _, fwo, _, _, w1, _, w2, _, _ = self.dram
        wait_for("wqkv")
        sp.dma_start(self.wqkv[:, :], wqkv[layer]).then_inc(self.wqkv_in, 16)
        wait_for("fwo")
        sp.dma_start(self.fwo[:, :, :], fwo[layer].rearrange("(c p) n -> p c n", p=P)).then_inc(self.w_in, 16)
        wait_for("w1")
        sp.dma_start(self.w1[:, :], w1[layer]).then_inc(self.w_in, 16)
        wait_for("w2")
        for f, (f0, m) in enumerate(HID_TILES):
            sp.dma_start(self.w2[0:m, f, :], w2[layer][f0:f0 + m, :]).then_inc(self.w_in, 16)

    def load_first(self, sp):
        _, q_scale, k_scale, _, ln_g, ln_b, _, b1, _, b2, rot = self.dram
        self.load_layer(sp, 0, lambda name: None)
        sp.dma_start(self.rot[:, :, :, :, :].rearrange("p a b t d -> p (a b t d)"), rot).then_inc(self.tab_in, 16)
        sp.wait_ge(self.vec_zero, 1)
        for layer in range(DEPTH):
            for n, scale in enumerate((q_scale, k_scale)):
                sp.dma_start(self.qk_gain[:, layer, n, :], scale[layer].partition_broadcast(P)) \
                    .then_inc(self.vec_in, 16)
            for n, src in enumerate((ln_g, ln_b, b2)):
                sp.dma_start(self.vec[:, layer, n:n + 1], src[layer].unsqueeze(1)).then_inc(self.vec_in, 16)
            for part in range(2):
                for f, (f0, m) in enumerate(HID_TILES):
                    n = 3 + part * len(HID_TILES) + f
                    sp.dma_start(self.vec[0:m, layer, n:n + 1],
                                 b1[layer][part * HID + f0:part * HID + f0 + m].unsqueeze(1)).then_inc(self.vec_in, 16)


def normalise_input(nc, keep, x, weights):
    x_tok, xn_parts, res, ident, psum = (keep[n] for n in ("x_tok", "xn_parts", "res", "ident", "psum"))
    x_by_chunk = x.rearrange("b t d -> (b t) d").rearrange("(h c s) d -> h s c d", h=2, s=CT)
    with ExitStack() as ctx:
        def sb(name, shape):
            return ctx.enter_context(nc.sbuf_tensor(name, shape, FP32))

        def sem(name):
            return ctx.enter_context(nc.semaphore(name))

        xc = sb("xc", [P, CHUNKS, DIM])
        xsq = sb("xsq", [P, CHUNKS, DIM])
        stat = sb("stat", [P, 4, CHUNKS])
        x_in = sem("x_in")
        ident_zero, ident_ready = sem("ident_zero"), sem("ident_ready")
        stat_step, rsqrt_step = sem("stat_step"), sem("input_rsqrt_step")
        centred, squared, xn_ready = sem("centred"), sem("squared"), sem("xn_ready")
        turned, xn_t_ready, high_ready = sem("turned"), sem("xn_t_ready"), sem("high_ready")
        block = ctx.enter_context(nc.Block())

        def per_token(row):
            return stat[:, row, :].unsqueeze(2).broadcast_to([P, CHUNKS, DIM])

        @block.sync
        def _(sp):
            for h in range(2):
                sp.dma_start(x_tok[h * HALF:(h + 1) * HALF, :, :], x_by_chunk[h]).then_inc(x_in, 16)
            weights.load_first(sp)

        @block.gpsimd
        def _(pool):
            nc.gpsimd.memset(weights.vec[:, :, :], 0.0).then_inc(weights.vec_zero, 1)
            nc.gpsimd.memset(ident[:, :], 0.0).then_inc(ident_zero, 1)
            pool.wait_ge(ident_zero, 1)
            nc.gpsimd.affine_select(out=ident[:, :], in_=ident[:, :], compare_op=ALU.not_equal, fill=1.0,
                                    base=0, pattern=[[-1, P]], channel_multiplier=1).then_inc(ident_ready, 1)

        @block.vector
        def _(dve):
            dve.wait_ge(x_in, 32)
            nc.vector.reduce_sum(stat[:, 0, :], x_tok[:, :, :], AX_X).then_inc(stat_step, 1)
            dve.wait_ge(stat_step, 1)
            nc.vector.tensor_scalar(stat[:, 1, :], stat[:, 0, :], 1.0 / DIM, None, ALU.mult).then_inc(stat_step, 1)
            dve.wait_ge(stat_step, 2)
            nc.vector.tensor_tensor(xc[:, :, :], x_tok[:, :, :], per_token(1), ALU.subtract).then_inc(centred, 1)
            dve.wait_ge(squared, 1)
            nc.vector.reduce_sum(stat[:, 2, :], xsq[:, :, :], AX_X).then_inc(stat_step, 1)
            dve.wait_ge(stat_step, 3)
            nc.vector.tensor_scalar(stat[:, 3, :], stat[:, 2, :], 1.0 / DIM, LN_EPS, ALU.mult, ALU.add) \
                .then_inc(stat_step, 1)
            dve.wait_ge(stat_step, 4)
            rsqrt(nc, dve, stat[:, 0, :], stat[:, 3, :], stat[:, 1, :], rsqrt_step, 0)
            nc.vector.tensor_tensor(xc[:, :, :], xc[:, :, :], per_token(0), ALU.mult).then_inc(xn_ready, 1)
            dve.wait_ge(high_ready, 1)
            nc.vector.tensor_tensor(xn_parts[:, 1, :], res[:, :, :].rearrange("p b t -> p (b t)"),
                                    xn_parts[:, 0, :], ALU.subtract)

        @block.scalar
        def _(act):
            act.wait_ge(centred, 1)
            nc.scalar.activation(xsq[:, :, :], xc[:, :, :], ACT.Square).then_inc(squared, 1)
            flat = res[:, :, :].rearrange("p b t -> p (b t)")
            by_chunk = flat.rearrange("p (h c s) -> p c h s", h=2, s=CT)
            for g in range(CHUNKS // 4):
                act.wait_ge(turned, g + 1)
                src = psum[:, g, :].rearrange("p (c h s) -> p c h s", c=4, h=2)
                nc.scalar.activation(by_chunk[:, 4 * g:4 * g + 4], src, ACT.Copy).then_inc(xn_t_ready, 1)
            act.wait_ge(xn_t_ready, CHUNKS // 4)
            nc.scalar.activation(xn_parts[:, 0, :], flat, ACT.Copy).then_inc(high_ready, 1)

        @block.tensor
        def _(pe):
            pe.wait_ge(ident_ready, 1)
            pe.wait_ge(xn_ready, 1)
            for c in range(CHUNKS):
                turn = nc.tensor.transpose(psum[:, c // 4, (c % 4) * P:(c % 4 + 1) * P], xc[:, c, :], ident[:, :])
                if c % 4 == 3:
                    turn.then_inc(turned, 1)


def gate_branch(nc, keep, weights, lin_w):
    res, gate, ident, psum = (keep[n] for n in ("res", "gate", "ident", "psum"))
    SHARES = UNITS // LANES
    with ExitStack() as ctx:
        def sb(name, shape):
            return ctx.enter_context(nc.sbuf_tensor(name, shape, FP32))

        def sem(name):
            return ctx.enter_context(nc.semaphore(name))

        wqkv_sb, fwo_sb, w1_sb, w2_sb = weights.wqkv, weights.fwo, weights.w1, weights.w2
        qk_gain, vec_all, rot_sb = weights.qk_gain, weights.vec, weights.rot
        vec_in, tab_in, wqkv_in, w_in = weights.vec_in, weights.tab_in, weights.wqkv_in, weights.w_in
        vec_sb = sb("vec_sb", [P, weights.VECS])
        lng_sb, lnb_sb, b2_sb = (vec_sb[:, n:n + 1] for n in range(3))
        b1_sb = vec_sb[:, 3:].rearrange("p (a f) -> p a f", a=2)
        rot_gain = sb("rot_gain", [P, 2, 2, QT, FD])
        largest = sb("largest", [P, SHARES, 3])
        largest_of = sb("largest_of", [P, 3])
        mean_w = sb("mean_w", [P, P])
        mask = sb("mask", [P, 2, KEYS])
        h_t = sb("h_t", [P, LANES, SEQ])
        v_tok = sb("v_tok", [P, LANES, QT, INNER])
        k_t = sb("k_t", [P, LANES, FH // 2, WIN + SEQ])
        o_t = [sb("o_t", [P, FH // 2, SEQ]), gate[:, :, :].rearrange("p (n c) d -> p n (c d)", n=FH // 2)]
        qk_work = sb("qk_work", [P, 5 * 2 * INNER])
        qk_sq, qk_raw, qk_cos, qk_sin, qk_rot = (
            qk_work[:, n * 2 * INNER:(n + 1) * 2 * INNER].rearrange("p (h d) -> p h d", d=FD) for n in range(5))
        q_t = sb("q_t", [P, FH, P])
        qk_stat = sb("qk_stat", [P, 4, 2 * FH])
        s_mask = sb("s_mask", [P, FH, KEYS])
        prob = sb("prob", [P, FH, 2 * P])
        s_stat = sb("s_stat", [P, 4, FH])
        ln_stat = sb("ln_stat", [P, 3, QT])
        p_both = sb("p_both", [P, 2, FH, P])
        p_own, p_prev = p_both[:, 0], p_both[:, 1]
        h2 = [h_t[:, l, :] for l in range(LANES)]
        spare = [qk_work, p_both[:, :, :, :].rearrange("p a h n -> p (a h n)")]
        hc, hsq = ([spare[l][:, n * SEQ:(n + 1) * SEQ] for l in range(LANES)] for n in range(2))
        diag = hsq
        ffn = [qk_work[:, 4 * SEQ:7 * SEQ].rearrange("p (f n) -> p f n", n=SEQ),
               s_mask[:, :, :].rearrange("p h k -> p (h k)").rearrange("p (f n) -> p f n", n=SEQ)]

        consts, share_ready, largest_ready = sem("consts"), sem("share_ready"), sem("largest_ready")
        gain_ready = sem("gain_ready")
        h_ready, qkv_ready = sem("h_ready"), sem("qkv_ready")
        sq_ready, v_ready, ss_ready, floor_ready = sem("sq_ready"), sem("v_ready"), sem("ss_ready"), sem("floor_ready")
        raw_ready, cos_ready, sin_ready, sum_ready, rot_ready = (
            sem("raw_ready"), sem("cos_ready"), sem("sin_ready"), sem("sum_ready"), sem("rot_ready"))
        qk_turned, qt_ready, kt_ready = sem("qk_turned"), sem("qt_ready"), sem("kt_ready")
        sim_ready, masked_ready, negmax_ready = sem("sim_ready"), sem("masked_ready"), sem("negmax_ready")
        exp_ready, rsum_ready, prob_ready = sem("exp_ready"), sem("rsum_ready"), sem("prob_ready")
        p_turned, p_kept, prev_kept = sem("p_turned"), sem("p_kept"), sem("prev_kept")
        pv_ready, ot_ready, wo_ready = sem("pv_ready"), sem("ot_ready"), sem("wo_ready")
        res_mid, h2_ready, mean_ready, hc_ready = sem("res_mid"), sem("h2_ready"), sem("mean_ready"), sem("hc_ready")
        hsq_ready, var_ready, rstd_ready, hn_ready = (sem("hsq_ready"), sem("var_ready"),
                                                      sem("rstd_ready"), sem("hn_ready"))
        hidden_ready, hln_ready, gelu_ready, ffn_ready = (sem("hidden_ready"), sem("hln_ready"),
                                                          sem("gelu_ready"), sem("ffn_ready"))
        rsqrt_step, ln_rsqrt_step, diag_ready = sem("rsqrt_step"), sem("ln_rsqrt_step"), sem("diag_ready")
        var_kept = sem("var_kept")
        w2_ready, unit_done = sem("w2_ready"), sem("unit_done")
        silu_ready, gate_turned, gate_ready = sem("silu_ready"), sem("gate_turned"), sem("gate_ready")
        block = ctx.enter_context(nc.Block())

        NF = len(HID_TILES)
        VEC_DMAS, W_DMAS = weights.VEC_DMAS, weights.W_DMAS
        PAIRS_OF_SEQ = BATCH // LANES
        SPLIT_F = 1
        TILES = LANES * QT
        STEPS = 2 * TILES
        HH = FH // 2
        LANE_BANK = [2, 7]
        G_BANK = [0, 3, 5]
        A_BANK = [1, 4, 6]

        def slot_bank(s):
            return 3 + 2 * (s % 2)

        TURN_BANK = slot_bank(0)

        def heads(s):
            return slice((s % 2) * HH, (s % 2 + 1) * HH)

        @block.sync
        def _(sp):
            for n, src in enumerate(lin_w):
                sp.dma_start(raw_weights(keep, n), src).then_inc(keep["lin_w_in"], 16)
            with sp.Fori(1, DEPTH) as layer:
                before = layer * PAIRS_OF_SEQ - 1
                last_use = {"wqkv": (qkv_ready, nth(before, TILES, TILES - 1)),
                            "fwo": (wo_ready, nth(before, LANES, LANES - 1)),
                            "w1": (hidden_ready, nth(before, LANES * NF, LANES * NF - 1)),
                            "w2": (w2_ready, nth(before, LANES, LANES - 1))}
                weights.load_layer(sp, layer, lambda name: sp.wait_ge(*last_use[name]))

        @block.gpsimd
        def _(pool):
            nc.gpsimd.memset(mean_w[:, :], 1.0 / DIM).then_inc(consts, 1)
            nc.gpsimd.memset(k_t[:, :, :, 0:WIN], 0.0).then_inc(consts, 1)
            nc.gpsimd.memset(prob[:, :, 0:WIN], 0.0).then_inc(consts, 1)
            nc.gpsimd.memset(mask[:, :, :], 0.0).then_inc(consts, 1)
            nc.gpsimd.memset(q_t[:, :, :], 0.0).then_inc(consts, 1)
            pool.wait_ge(consts, 5)
            nc.gpsimd.affine_select(out=mask[:, :, :], in_=mask[:, :, :], compare_op=ALU.is_ge, fill=MASKED,
                                    base=0, pattern=[[0, 2], [1, KEYS]], channel_multiplier=-1).then_inc(consts, 1)
            pool.wait_ge(consts, 6)
            nc.gpsimd.affine_select(out=mask[:, :, :], in_=mask[:, :, :], compare_op=ALU.is_ge, fill=MASKED,
                                    base=WIN, pattern=[[0, 2], [-1, KEYS]], channel_multiplier=1).then_inc(consts, 1)
            pool.wait_ge(consts, 7)
            nc.gpsimd.memset(mask[:, 0, 0:WIN], MASKED).then_inc(consts, 1)

            with pool.Fori(0, UNITS // LANES) as u:
                def rotate(g):
                    pool.wait_ge(raw_ready, nth(u, TILES, g))
                    if g:
                        pool.wait_ge(sum_ready, nth(u, TILES, g - 1))
                    for half in range(2):
                        to = slice(half * 32, half * 32 + 32)
                        of = slice(32 - half * 32, 64 - half * 32)
                        table = rot_gain[:, 1, :, g // LANES, to].unsqueeze(2).broadcast_to([P, 2, FH, 32])
                        part = nc.gpsimd.tensor_tensor(
                            qk_sin[:, :, to].rearrange("p (a h) d -> p a h d", a=2),
                            qk_raw[:, :, of].rearrange("p (a h) d -> p a h d", a=2), table, ALU.mult)
                    part.then_inc(sin_ready, 1)

                def add_parts(g):
                    pool.wait_ge(cos_ready, nth(u, TILES, g))
                    pool.wait_ge(sin_ready, nth(u, TILES, g))
                    nc.gpsimd.tensor_tensor(qk_cos, qk_cos, qk_sin, ALU.add).then_inc(sum_ready, 1)

                def scale(s):
                    pool.wait_ge(rsum_ready, nth(u, STEPS, s))
                    nc.gpsimd.tensor_tensor(prob[:, heads(s), WIN:], prob[:, heads(s), WIN:],
                                            s_stat[:, 3, heads(s)].unsqueeze(2).broadcast_to([P, HH, KEYS]),
                                            ALU.mult).then_inc(prob_ready, 1)

                rotate(0)
                add_parts(0)
                rotate(1)
                for g in range(TILES):
                    scale(2 * g)
                    if g + 1 < TILES:
                        add_parts(g + 1)
                    scale(2 * g + 1)
                    if g + 2 < TILES:
                        rotate(g + 2)
            pool.wait_ge(largest_ready, 1)
            nc.gpsimd.partition_all_reduce(keep["peak"][:, 0:3], largest_of[:, :], P, REDUCE_MAX)

        @block.scalar
        def _(act):
            act.wait_ge(consts, 8)

            def square_and_values(u, g):
                act.wait_ge(qkv_ready, nth(u, TILES, g))
                if g:
                    act.wait_ge(cos_ready, nth(u, TILES, g - 1))
                    act.wait_ge(sin_ready, nth(u, TILES, g - 1))
                    act.wait_ge(ss_ready, nth(u, TILES, g - 1))
                qk = psum[:, 0:2, :].rearrange("p a n -> p (a n)")
                nc.scalar.activation(qk_raw.rearrange("p h d -> p (h d)"), qk, ACT.Copy).then_inc(raw_ready, 1)
                nc.scalar.activation(qk_sq.rearrange("p h d -> p (h d)"), qk, ACT.Square).then_inc(sq_ready, 1)
                nc.scalar.activation(v_tok[:, g % LANES, g // LANES, :], psum[:, 2, :], ACT.Copy).then_inc(v_ready, 1)

            def keep_turned_q(u, g):
                act.wait_ge(qk_turned, nth(u, TILES, g))
                for odd in range(2):
                    rows = slice(odd * HALF, (odd + 1) * HALF)
                    last = nc.scalar.activation(q_t[rows, odd::2, :],
                                                psum[rows, TURN_BANK, :].rearrange("p (h n) -> p h n", n=P), ACT.Copy)
                last.then_inc(qt_ready, 1)

            def exponentials(u, s):
                act.wait_ge(negmax_ready, nth(u, STEPS, s))
                for h in range(heads(s).start, heads(s).stop):
                    e = nc.scalar.activation(prob[:, h, WIN:], s_mask[:, h, :], ACT.Exp,
                                             bias=s_stat[:, 0, h:h + 1],
                                             accum_out=s_stat[:, 2, h:h + 1])
                e.then_inc(exp_ready, 1)

            def keep_turned_p(u, s):
                act.wait_ge(p_turned, nth(u, STEPS, s))
                own = nc.scalar.activation(p_own[:, heads(s), :].rearrange("p h n -> p (h n)"),
                                           psum[:, slot_bank(s), :], ACT.Copy)
                if s // 2 >= LANES and s % 2:
                    own = nc.scalar.activation(p_prev[:, heads(s), :].rearrange("p h n -> p (h n)"),
                                               psum[:, slot_bank(s) + 1, :], ACT.Copy)
                own.then_inc(p_kept, 1)

            def square_centred(u, l):
                act.wait_ge(hc_ready, nth(u, LANES, l))
                nc.scalar.activation(hsq[l], hc[l], ACT.Square).then_inc(hsq_ready, 1)

            def gain_and_bias(u, l):
                act.wait_ge(hn_ready, nth(u, LANES, l))
                nc.scalar.activation(h2[l], hc[l], ACT.Identity, bias=lnb_sb[:, 0:1],
                                     scale=lng_sb[:, 0:1]).then_inc(hln_ready, 1)

            def gelu(u, l, tiles=range(NF)):
                for f in tiles:
                    m = HID_TILES[f][1]
                    act.wait_ge(hidden_ready, nth(u, LANES * NF, l * NF + f))
                    nc.scalar.activation(ffn[l][0:m, f, :], psum[0:m, G_BANK[f], :], ACT.Gelu,
                                         bias=b1_sb[0:m, 1, f:f + 1]).then_inc(gelu_ready, 1)

            with act.Fori(0, DEPTH) as layer:
                with act.Fori(0, PAIRS_OF_SEQ) as b:
                    u = layer * PAIRS_OF_SEQ + b
                    square_and_values(u, 0)
                    square_and_values(u, 1)
                    keep_turned_q(u, 0)
                    for g in range(TILES):
                        exponentials(u, 2 * g)
                        exponentials(u, 2 * g + 1)
                        keep_turned_p(u, 2 * g)
                        if g + 2 < TILES:
                            square_and_values(u, g + 2)
                        if g + 1 < TILES:
                            keep_turned_q(u, g + 1)
                        keep_turned_p(u, 2 * g + 1)
                    square_centred(u, 0)
                    square_centred(u, 1)
                    gain_and_bias(u, 0)
                    gelu(u, 0, range(SPLIT_F))
                    gain_and_bias(u, 1)
                    gelu(u, 0, range(SPLIT_F, NF))
                    gelu(u, 1)
            act.wait_ge(unit_done, UNITS)
            by_chunk = res[:, :, :].rearrange("p b t -> p (b t)").rearrange("p (h c s) -> p c h s", h=2, s=CT)
            chunks = v_tok[:, 0].rearrange("p b t -> p (b t)").rearrange("p (c h s) -> p c h s", h=2, s=CT)
            nc.scalar.activation(chunks, by_chunk, ACT.Silu).then_inc(silu_ready, 1)
            for g in range(CHUNKS // 4):
                act.wait_ge(gate_turned, g + 1)
                nc.scalar.activation(gate[:, 4 * g:4 * g + 4, :].rearrange("p c n -> p (c n)"), psum[:, g, :],
                                     ACT.Copy).then_inc(gate_ready, 1)

        @block.vector
        def _(dve):
            dve.wait_ge(tab_in, 16)
            dve.wait_ge(vec_in, VEC_DMAS * 16)
            shares = keep["work"][:, 0:3 * LH * LD].rearrange("p (u n c) -> p u n c", u=SHARES, n=3)
            assert NF == 3
            dve.wait_ge(consts, 8)

            def shift_into(dst, src):
                nc.vector.tensor_copy(dst[0:HALF, :], src[0:HALF])
                nc.vector.memset(dst[HALF:P, 0:1], 0.0)
                return nc.vector.tensor_copy(dst[HALF:P, 1:SEQ], src[HALF:P, 0:SEQ - 1])

            def sum_squares(u, g):
                dve.wait_ge(sq_ready, nth(u, TILES, g))
                nc.vector.reduce_sum(qk_stat[:, 0, :], qk_sq, AX_X).then_inc(ss_ready, 1)

            def inverse_norms(u, g):
                dve.wait_ge(ss_ready, nth(u, TILES, g))
                nc.vector.tensor_scalar(qk_stat[:, 2, :], qk_stat[:, 0, :], NORM_FLOOR_SQ, None, ALU.max) \
                    .then_inc(floor_ready, 1)
                dve.wait_ge(floor_ready, nth(u, TILES, g))
                rsqrt(nc, dve, qk_stat[:, 1, :], qk_stat[:, 2, :], qk_stat[:, 3, :], rsqrt_step,
                      (u * TILES + g) * RSQRT_STEPS)

            def cosine_part(u, g):
                dve.wait_ge(raw_ready, nth(u, TILES, g))
                table = rot_gain[:, 0, :, g // LANES, :].unsqueeze(2).broadcast_to([P, 2, FH, FD])
                nc.vector.tensor_tensor(qk_cos.rearrange("p (a h) d -> p a h d", a=2),
                                        qk_raw.rearrange("p (a h) d -> p a h d", a=2), table,
                                        ALU.mult).then_inc(cos_ready, 1)

            def normalise(u, g):
                dve.wait_ge(sum_ready, nth(u, TILES, g))
                nc.vector.tensor_tensor(qk_rot, qk_cos, qk_stat[:, 1, :].unsqueeze(2).broadcast_to([P, 2 * FH, FD]),
                                        ALU.mult).then_inc(rot_ready, 1)

            def mask_and_max(u, s):
                t = s // 2 // LANES
                dve.wait_ge(sim_ready, nth(u, STEPS, s))
                banks = psum[:, slot_bank(s):slot_bank(s) + 2, 0:2 * KEYS].rearrange("p a (h k) -> p a h k", k=KEYS)
                nc.vector.tensor_tensor(
                    s_mask[:, heads(s), :].rearrange("p (a h) k -> p a h k", h=2), banks,
                    mask[:, min(t, 1), :].unsqueeze(1).unsqueeze(1).broadcast_to([P, 2, 2, KEYS]),
                    ALU.add).then_inc(masked_ready, 1)
                dve.wait_ge(masked_ready, nth(u, STEPS, s))
                nc.vector.tensor_reduce(s_stat[:, 0, heads(s)], s_mask[:, heads(s), :], AX_X, ALU.max,
                                        negate=True).then_inc(negmax_ready, 1)

            def inverse_sums(u, s):
                dve.wait_ge(exp_ready, nth(u, STEPS, s))
                nc.vector.reciprocal(s_stat[:, 3, heads(s)], s_stat[:, 2, heads(s)]).then_inc(rsum_ready, 1)

            def keep_turned_k(u, g):
                lane, t = g % LANES, g // LANES
                dve.wait_ge(qk_turned, nth(u, TILES, g))
                nc.vector.tensor_copy(k_t[:, lane, :, WIN + t * P:WIN + (t + 1) * P],
                                      psum[:, TURN_BANK + 1, :].rearrange("p (h n) -> p h n", n=P)).then_inc(kt_ready, 1)

            def keep_prev(u, g):
                if g >= LANES:
                    s = 2 * g
                    dve.wait_ge(p_turned, nth(u, STEPS, s))
                    nc.vector.tensor_copy(p_prev[:, heads(s), :].rearrange("p h n -> p (h n)"),
                                          psum[:, slot_bank(s) + 1, :]).then_inc(prev_kept, 1)

            def keep_outputs(u, s):
                g = s // 2
                lane, t = g % LANES, g // LANES
                dve.wait_ge(pv_ready, nth(u, STEPS, s))
                pairs = slice((s % 2) * HH // 2, (s % 2 + 1) * HH // 2)
                nc.vector.tensor_copy(o_t[lane][:, pairs, t * P:(t + 1) * P],
                                      psum[:, 7, :].rearrange("p (h n) -> p h n", n=P)[:, pairs]).then_inc(ot_ready, 1)

            def add_attention(u, l, x):
                dve.wait_ge(wo_ready, nth(u, LANES, l))
                nc.vector.tensor_tensor(x, x, psum[:, LANE_BANK[l], :], ALU.add).then_inc(res_mid, 1)
                wait_alone(dve, res_mid, nth(u, LANES, l))
                shift_into(h2[l], x).then_inc(h2_ready, 1)

            def centre(u, l):
                dve.wait_ge(mean_ready, nth(u, LANES, l))
                nc.vector.tensor_tensor(hc[l], h2[l], psum[:, LANE_BANK[l], :], ALU.subtract).then_inc(hc_ready, 1)

            def inverse_deviation(u, l):
                dve.wait_ge(var_ready, nth(u, LANES, l))
                nc.vector.tensor_scalar(ln_stat[:, 0, :], psum[:, LANE_BANK[l], 0:QT], LN_EPS, None, ALU.add) \
                    .then_inc(var_kept, 1)
                dve.wait_ge(var_kept, nth(u, LANES, l))
                rsqrt(nc, dve, ln_stat[:, 1, :], ln_stat[:, 0, :], ln_stat[:, 2, :], ln_rsqrt_step,
                      (u * LANES + l) * RSQRT_STEPS)
                nc.vector.scalar_tensor_tensor(
                    out=diag[l].rearrange("p (t n) -> p t n", n=P),
                    in0=ln_stat[:, 1, :].unsqueeze(2).broadcast_to([P, QT, P]), scalar=float(DIM),
                    in1=ident[:, :].unsqueeze(1).broadcast_to([P, QT, P]), op0=ALU.mult, op1=ALU.mult) \
                    .then_inc(diag_ready, 1)

            def divide_by_deviation(u, l):
                dve.wait_ge(rstd_ready, nth(u, LANES, l))
                nc.vector.tensor_tensor(hc[l], hc[l], psum[:, LANE_BANK[l], :], ALU.mult).then_inc(hn_ready, 1)

            def apply_gate(u, l, tiles):
                for f in tiles:
                    m = HID_TILES[f][1]
                    dve.wait_ge(gelu_ready, nth(u, LANES * NF, l * NF + f))
                    nc.vector.scalar_tensor_tensor(out=ffn[l][0:m, f, :], in0=psum[0:m, A_BANK[f], :],
                                                   scalar=b1_sb[0:m, 0, f:f + 1], in1=ffn[l][0:m, f, :],
                                                   op0=ALU.add, op1=ALU.mult).then_inc(ffn_ready, 1)

            def add_feed_forward(u, l, x):
                dve.wait_ge(w2_ready, nth(u, LANES, l))
                nc.vector.scalar_tensor_tensor(out=x, in0=psum[:, LANE_BANK[l], :], scalar=b2_sb[:, 0:1],
                                               in1=x, op0=ALU.add, op1=ALU.add).then_inc(unit_done, 1)

            with dve.Fori(0, DEPTH) as layer:
                nc.vector.tensor_copy(vec_sb[:, :], vec_all[:, layer, :])
                for n in range(2):
                    gain = qk_gain[:, layer, n, :].unsqueeze(1)
                    nc.vector.tensor_tensor(rot_gain[:, 0, n], rot_sb[:, 0, n], gain.broadcast_to([P, QT, FD]), ALU.mult)
                    for half in range(2):
                        to = slice(half * 32, half * 32 + 32)
                        of = slice(32 - half * 32, 64 - half * 32)
                        last = nc.vector.tensor_tensor(rot_gain[:, 1, n, :, to], rot_sb[:, 1, n, :, to],
                                                       gain[:, :, of].broadcast_to([P, QT, 32]), ALU.mult)
                last.then_inc(gain_ready, 1)
                wait_alone(dve, gain_ready, layer + 1)
                with dve.Fori(0, PAIRS_OF_SEQ) as b:
                    u = layer * PAIRS_OF_SEQ + b
                    x = [res[:, b * LANES + l, :] for l in range(LANES)]
                    for l in range(LANES):
                        shift_into(h_t[:, l, :], x[l]).then_inc(h_ready, 1)
                    cosine_part(u, 0)
                    sum_squares(u, 0)
                    inverse_norms(u, 0)
                    normalise(u, 0)
                    keep_turned_k(u, 0)
                    for g in range(TILES):
                        mask_and_max(u, 2 * g)
                        if g:
                            keep_outputs(u, 2 * g - 1)
                        if g + 1 < TILES:
                            cosine_part(u, g + 1)
                        inverse_sums(u, 2 * g)
                        mask_and_max(u, 2 * g + 1)
                        if g + 1 < TILES:
                            sum_squares(u, g + 1)
                        keep_prev(u, g)
                        inverse_sums(u, 2 * g + 1)
                        if g + 1 < TILES:
                            inverse_norms(u, g + 1)
                            normalise(u, g + 1)
                        else:
                            add_attention(u, 0, x[0])
                        keep_outputs(u, 2 * g)
                        if g + 1 < TILES:
                            keep_turned_k(u, g + 1)
                    keep_outputs(u, STEPS - 1)
                    centre(u, 0)
                    add_attention(u, 1, x[1])
                    inverse_deviation(u, 0)
                    centre(u, 1)
                    divide_by_deviation(u, 0)
                    inverse_deviation(u, 1)
                    apply_gate(u, 0, range(SPLIT_F))
                    divide_by_deviation(u, 1)
                    apply_gate(u, 0, range(SPLIT_F, NF))
                    wait_alone(dve, keep["lin_w_in"], 3 * 16)
                    for f in range(NF):
                        nc.vector.tensor_reduce(largest[:, u, f:f + 1], shares[:, u, f], AX_X, ALU.max,
                                                apply_absolute_value=True).then_inc(share_ready, 1)
                        apply_gate(u, 1, (f,))
                    add_feed_forward(u, 0, x[0])
                    add_feed_forward(u, 1, x[1])
                    wait_alone(dve, unit_done, nth(u, LANES, LANES - 1))
            dve.wait_ge(share_ready, SHARES * NF)
            shares_of = largest[:, :, :].rearrange("p u n -> p (u n)").rearrange("p (n s) -> p n s", n=3)
            nc.vector.tensor_reduce(largest_of[:, :], shares_of, AX_X, ALU.max).then_inc(largest_ready, 1)

        @block.tensor
        def _(pe):
            pe.wait_ge(consts, 8)

            def project(u, g):
                lane, t = g % LANES, g // LANES
                if g < LANES:
                    pe.wait_ge(h_ready, nth(u, LANES, lane))
                if g:
                    pe.wait_ge(sq_ready, nth(u, TILES, g - 1))
                    pe.wait_ge(v_ready, nth(u, TILES, g - 1))
                for n in range(3):
                    last = nc.tensor.matmul(psum[:, n, :], h_t[:, lane, t * P:(t + 1) * P],
                                            wqkv_sb[:, n * INNER:(n + 1) * INNER], start=True, stop=True)
                last.then_inc(qkv_ready, 1)

            def turn_qk(u, g):
                pe.wait_ge(rot_ready, nth(u, TILES, g))
                for n in range(2):
                    for pair in range(FH // 2):
                        pairs = qk_rot[:, n * FH + 2 * pair:n * FH + 2 * pair + 2, :]
                        last = nc.tensor.transpose(psum[:, TURN_BANK + n, pair * P:(pair + 1) * P],
                                                   pairs.rearrange("p h d -> p (h d)"), ident[:, :])
                last.then_inc(qk_turned, 1)

            def turned_p_kept(u, s):
                pe.wait_ge(p_kept, nth(u, STEPS, s))
                if s // 2 >= LANES and s % 2 == 0:
                    pe.wait_ge(prev_kept, nth(u, TILES - LANES, s // 2 - LANES))

            def scores(u, s):
                g = s // 2
                lane, t = g % LANES, g // LANES
                pe.wait_ge(qt_ready, nth(u, TILES, g))
                pe.wait_ge(kt_ready, nth(u, TILES, g))
                if s >= 2:
                    turned_p_kept(u, s - 2)
                for n in range(HH):
                    h = (s % 2) * HH + n
                    last = nc.tensor.matmul(psum[:, slot_bank(s) + n // 2, (n % 2) * KEYS:(n % 2 + 1) * KEYS],
                                            q_t[:, h, :], k_t[:, lane, h // 2, t * P:t * P + KEYS],
                                            start=True, stop=True)
                last.then_inc(sim_ready, 1)

            def turn_probabilities(u, s):
                pe.wait_ge(prob_ready, nth(u, STEPS, s))
                for n in range(HH):
                    h = (s % 2) * HH + n
                    last = nc.tensor.transpose(psum[:, slot_bank(s), n * P:(n + 1) * P], prob[:, h, P:2 * P], ident[:, :])
                    if s // 2 >= LANES:
                        last = nc.tensor.transpose(psum[:, slot_bank(s) + 1, n * P:(n + 1) * P], prob[:, h, 0:P],
                                                   ident[:, :])
                last.then_inc(p_turned, 1)

            def times_values(u, s):
                g = s // 2
                lane, t = g % LANES, g // LANES
                turned_p_kept(u, s)
                if s:
                    pe.wait_ge(ot_ready, nth(u, STEPS, s - 1))
                for n in range(HH):
                    h = (s % 2) * HH + n
                    o = psum[(h % 2) * HALF:(h % 2 + 1) * HALF, 7, (h // 2) * P:(h // 2 + 1) * P]
                    last = nc.tensor.matmul(o, v_tok[:, lane, t, h * FD:(h + 1) * FD], p_own[:, h, :],
                                            start=True, stop=(t == 0))
                    if t:
                        last = nc.tensor.matmul(o, v_tok[:, lane, t - 1, h * FD:(h + 1) * FD], p_prev[:, h, :],
                                                start=False, stop=True)
                last.then_inc(pv_ready, 1)

            def project_attention(u, l, layer):
                if l == 0:
                    pe.wait_ge(w_in, nth(layer, W_DMAS * 16, W_DMAS * 16 - 1))
                pe.wait_ge(ot_ready, nth(u, STEPS, 2 * (TILES - LANES + l) + 1))
                for pair in range(FH // 2):
                    last = nc.tensor.matmul(psum[:, LANE_BANK[l], :], fwo_sb[:, pair, :], o_t[l][:, pair, :],
                                            start=(pair == 0), stop=(pair == FH // 2 - 1))
                last.then_inc(wo_ready, 1)

            def average(of, ready, done, l):
                pe.wait_ge(*ready)
                nc.tensor.matmul(psum[:, LANE_BANK[l], :], mean_w[:, :], of[l], start=True, stop=True).then_inc(done, 1)

            def variance(u, l):
                pe.wait_ge(hsq_ready, nth(u, LANES, l))
                for t in range(QT):
                    last = nc.tensor.matmul(psum[:, LANE_BANK[l], t:t + 1], hsq[l][:, t * P:(t + 1) * P],
                                            mean_w[:, 0:1], start=True, stop=True)
                last.then_inc(var_ready, 1)

            def hidden(u, l, tiles):
                pe.wait_ge(hln_ready, nth(u, LANES, l))
                for f in tiles:
                    f0, m = HID_TILES[f]
                    if l:
                        pe.wait_ge(ffn_ready, nth(u, LANES * NF, (l - 1) * NF + f))
                    nc.tensor.matmul(psum[0:m, G_BANK[f], :], w1_sb[:, HID + f0:HID + f0 + m], h2[l],
                                     start=True, stop=True)
                    nc.tensor.matmul(psum[0:m, A_BANK[f], :], w1_sb[:, f0:f0 + m], h2[l],
                                     start=True, stop=True).then_inc(hidden_ready, 1)

            def project_hidden(u, l):
                for f, (f0, m) in enumerate(HID_TILES):
                    pe.wait_ge(ffn_ready, nth(u, LANES * NF, l * NF + f))
                    last = nc.tensor.matmul(psum[:, LANE_BANK[l], :], w2_sb[0:m, f, :], ffn[l][0:m, f, :],
                                            start=(f == 0), stop=(f == NF - 1))
                last.then_inc(w2_ready, 1)

            with pe.Fori(0, DEPTH) as layer:
                wait_alone(pe, wqkv_in, nth(layer, 16, 15))
                with pe.Fori(0, PAIRS_OF_SEQ) as b:
                    u = layer * PAIRS_OF_SEQ + b
                    project(u, 0)
                    project(u, 1)
                    turn_qk(u, 0)
                    scores(u, 0)
                    for g in range(TILES):
                        scores(u, 2 * g + 1)
                        if g + 2 < TILES:
                            project(u, g + 2)
                        elif g + 1 == TILES:
                            project_attention(u, 0, layer)
                        turn_probabilities(u, 2 * g)
                        times_values(u, 2 * g)
                        turn_probabilities(u, 2 * g + 1)
                        if g + 1 < TILES:
                            turn_qk(u, g + 1)
                        else:
                            average(h2, (h2_ready, nth(u, LANES, 0)), mean_ready, 0)
                        if g + 1 < TILES:
                            scores(u, 2 * g + 2)
                        times_values(u, 2 * g + 1)
                    project_attention(u, 1, layer)
                    variance(u, 0)
                    average(h2, (h2_ready, nth(u, LANES, 1)), mean_ready, 1)
                    average(diag, (diag_ready, nth(u, LANES, 0)), rstd_ready, 0)
                    variance(u, 1)
                    hidden(u, 0, range(SPLIT_F))
                    average(diag, (diag_ready, nth(u, LANES, 1)), rstd_ready, 1)
                    hidden(u, 0, range(SPLIT_F, NF))
                    hidden(u, 1, range(NF))
                    project_hidden(u, 0)
                    project_hidden(u, 1)
            pe.wait_ge(silu_ready, 1)
            chunks = v_tok[:, 0].rearrange("p b (c n) -> p (b c) n", n=P)
            for c in range(CHUNKS):
                last = nc.tensor.transpose(psum[:, c // 4, (c % 4) * P:(c % 4 + 1) * P], chunks[:, c, :], ident[:, :])
                if c % 4 == 3:
                    last.then_inc(gate_turned, 1)


def raw_weights(keep, n):
    return keep["work"][:, n * LH * LD:(n + 1) * LH * LD]


def linear_branch(nc, keep, wo, bo, out):
    x_tok, xn_parts, gate, psum = (keep[n] for n in ("x_tok", "xn_parts", "gate", "psum"))
    peak, work = keep["peak"], keep["work"]
    PAIRS = LH // 2
    PROJ_GROUP = 1024 // (2 * ST)
    OUT_GROUP = 1024 // P
    NG = PAIRS // PROJ_GROUP
    NT = ST // OUT_GROUP
    SLOTS = 4
    SPLIT_ORDER = (1, 0, 2)
    HIGH, LOW = 0, 1
    PASSES = [(HIGH, HIGH), (HIGH, LOW), (LOW, HIGH)]
    USES = [("q", 0), ("q", 1), ("sum", 0), ("v", 0), ("out", 0), ("v", 1), ("out", 1), ("k", 0),
            ("out", 2), ("k", 1), ("out", 3), ("y", 0)]
    assert len(USES) % SLOTS == 0 and NG == 2 and NT == 4
    PER = {"k": NG, "v": NG, "sum": 1, "q": NG, "out": NT}
    AHEAD = {"k": 2, "v": 1, "sum": 1, "q": 1, "out": 0}

    def happens(kind, turn):
        if kind == "y":
            return turn >= PARTS
        return 0 <= turn + AHEAD[kind] < NSTEPS

    with ExitStack() as ctx:
        def sb(name, shape, dtype=FP32):
            return ctx.enter_context(nc.sbuf_tensor(name, shape, dtype))

        def sem(name):
            return ctx.enter_context(nc.semaphore(name))

        w_parts = sb("w_parts", [P, 3, 2, LH * LD], FP16)
        scale = sb("scale", [P, 3, 4])
        q_f = work[:, 0:ST * LH].rearrange("p (s i) -> p s i", i=LH)
        v_f = work[:, ST * LH:ST * 2 * LH].rearrange("p (s j) -> p s j", j=LH)
        o_s = work[:, ST * 2 * LH:ST * 2 * LH + 2 * PAIRS * P].rearrange("p (b j t) -> p b j t", b=2, t=P)
        wo_sb = sb("wo_sb", [P, PAIRS, DIM])
        bo_sb = sb("bo_sb", [P, DIM])
        pair_sum = sb("pair_sum", [P, 2, HALF])
        x_s = sb("x_s", [P, 4, 2, 2, ST], FP16)
        k_acc = sb("k_acc", [P, PROJ_GROUP, 2 * ST])
        k_heads = sb("k_heads", [P, 2 * ST])
        k_sum = sb("k_sum", [P, ST])
        q_parts = sb("q_parts", [P, 2, 2, ST, 2, LH], FP16)
        v_parts = sb("v_parts", [P, 2, 2, ST, LH + 2], FP16)
        denom = sb("denom", [P, 2, 2, OUT_GROUP])
        y_sb = sb("y_sb", [P, PARTS, DIM])
        y_step = sb("y_step", [P, 2, DIM])

        wo_in, consts = sem("lin_wo_in"), sem("lin_consts")
        scale_step, scale_ready = sem("scale_step"), sem("scale_ready")
        w_high_ready, w_low_ready = sem("w_high_ready"), sem("w_low_ready")
        x_ready = sem("x_ready")
        filled = {kind: sem(f"{kind}_filled") for kind in PER}
        read = {kind: sem(f"{kind}_read") for kind in PER}
        k_heads_ready = sem("k_heads_ready")
        q_scaled, q_high, q_low_a, q_low_b, v_high, v_low = (
            sem("q_scaled"), sem("q_high"), sem("q_low_a"), sem("q_low_b"), sem("v_high"), sem("v_low"))
        wo_scaled = sem("wo_scaled")
        denom_ready, recip_ready = sem("denom_ready"), sem("recip_ready")
        y_filled, y_ready, y_used, y_chain = sem("y_filled"), sem("y_ready"), sem("y_used"), sem("y_chain")
        o_ready, stored = sem("o_ready"), sem("stored")
        block = ctx.enter_context(nc.Block())

        def slot(kind, g):
            first = 2 * (USES.index((kind, g)) % SLOTS)
            width = 2 * ST if kind in ("q", "k", "v") else P
            return psum[:, first:first + 2, :].rearrange("p a (n c) -> p (a n) c", c=width)

        def heads_of(buffer, g):
            return buffer.rearrange("p s (a n) -> p s a n", a=2)[:, :, :, g * PROJ_GROUP:(g + 1) * PROJ_GROUP]

        def low_q_operands(buf, g, half):
            rows = slice(half * HALF, (half + 1) * HALF)
            return (heads_of(q_parts[rows, buf, LOW, :, half, :], g), heads_of(q_f[rows], g),
                    heads_of(q_parts[rows, buf, HIGH, :, half, :], g))

        def known(r, k):
            return 4 * (r if isinstance(r, int) else 1) + k

        def place(n):
            return (0, n) if n < 2 else ((n - 2) // 4, (n - 2) % 4 + 2)

        @block.sync
        def _(sp):
            rows = wo.rearrange("(ia ib ja jb) n -> jb ib ia ja n", ia=LH // 2, ib=2, ja=LH // 2, jb=2)
            for jb in range(2):
                for ib in range(2):
                    p0 = jb * HALF + ib * 32
                    sp.dma_start(wo_sb[p0:p0 + 32, :, :], rows[jb, ib]).then_inc(wo_in, 16)
            sp.dma_start(bo_sb[:, :], bo.partition_broadcast(P)).then_inc(wo_in, 16)
            out_by_chunk = out.rearrange("b t d -> (b t) d").rearrange("(h c s) d -> h c s d", h=2, s=CT)
            with sp.Fori(0, CHUNKS) as c:
                sp.wait_ge(o_ready, c + 1)
                for h in range(2):
                    sp.dma_start(out_by_chunk[h, c], x_tok[h * HALF:(h + 1) * HALF, c, :]).then_inc(stored, 16)
            sp.wait_ge(stored, CHUNKS * 2 * 16)

        @block.gpsimd
        def _(pool):
            by_chunk = xn_parts[:, :, :].rearrange("p a (h c e s) -> p a c e h s", h=2, c=CHUNKS, e=PARTS)

            def take_tokens(c, k):
                for part in (HIGH, LOW):
                    last = nc.gpsimd.tensor_copy(x_s[:, k % 4, part], by_chunk[:, part, c, k % PARTS])
                last.then_inc(x_ready, 1)

            for m in range(3):
                take_tokens(m // PARTS, m)
            nc.gpsimd.memset(pair_sum[:, :, :], 0.0).then_inc(consts, 1)
            nc.gpsimd.memset(v_parts[:, :, HIGH, :, LH:LH + 1], 1.0).then_inc(consts, 1)
            nc.gpsimd.memset(v_parts[:, :, LOW, :, LH:LH + 1], 0.0).then_inc(consts, 1)
            pool.wait_ge(consts, 3)
            for k, base in enumerate((0, -HALF)):
                nc.gpsimd.affine_select(out=pair_sum[:, :, :], in_=pair_sum[:, :, :], compare_op=ALU.not_equal,
                                        fill=1.0, base=base, pattern=[[0, 2], [-1, HALF]],
                                        channel_multiplier=1).then_inc(consts, 1)
                pool.wait_ge(consts, 4 + k)
            for half in range(2):
                for buf in range(2):
                    for part in (HIGH, LOW):
                        zeros = q_parts[half * HALF:(half + 1) * HALF, buf, part, :, 1 - half, :]
                        nc.gpsimd.memset(zeros, 0.0).then_inc(consts, 1)
                pool.wait_ge(consts, 3 + 2 + 4 * (half + 1))
            pool.nop().then_inc(y_used, 1)

            def lows(n, buf, first=False):
                if not first:
                    wait_alone(pool, v_low, nth(n - 1, NG, NG - 1))
                for g in range(NG):
                    wait_alone(pool, q_high, nth(n, 2 * NG, 2 * g + 1))
                    nc.gpsimd.tensor_tensor(*low_q_operands(buf, g, 1), ALU.subtract).then_inc(q_low_b, 1)
                    wait_alone(pool, q_low_b, nth(n, NG, g))
                for g in range(NG):
                    pool.wait_ge(v_high, nth(n, NG, g))
                    nc.gpsimd.tensor_tensor(heads_of(v_parts[:, buf, LOW, :, 0:LH], g), heads_of(v_f, g),
                                            heads_of(v_parts[:, buf, HIGH, :, 0:LH], g), ALU.subtract) \
                        .then_inc(v_low, 1)

            def finish(c):
                pool.wait_ge(y_ready, nth(c, PARTS, PARTS - 1))
                nc.gpsimd.tensor_tensor(y_step[:, 0, :], y_sb[:, 0, :], y_sb[:, 1, :], ALU.add).then_inc(y_chain, 1)
                pool.wait_ge(y_chain, nth(c, 3))
                pool.nop().then_inc(y_used, 1)
                nc.gpsimd.tensor_tensor(y_step[:, 1, :], y_step[:, 0, :], bo_sb[:, :], ALU.add).then_inc(y_chain, 1)
                pool.wait_ge(y_chain, nth(c, 3, 1))
                nc.gpsimd.tensor_tensor(y_step[:, 0, :], y_step[:, 1, :], gate[:, c, :], ALU.mult).then_inc(y_chain, 1)
                pool.wait_ge(y_chain, nth(c, 3, 2))
                nc.gpsimd.tensor_tensor(x_tok[:, c, :], y_step[:, 0, :], x_tok[:, c, :], ALU.add).then_inc(o_ready, 1)

            lows(0, 0, True)
            pool.wait_ge(wo_in, 5 * 16)

            def turn(r, k):
                n = known(r, k)
                if n + 3 < NSTEPS:
                    if n >= 1:
                        wait_alone(pool, filled["v"], nth(4 * r + k - 1, NG, NG - 1))
                    take_tokens(2 * r + (k + 3) // PARTS, k + 3)
                    wait_alone(pool, x_ready, 4 * r + k + 4)
                if n % PARTS == 0 and n >= 2 * PARTS:
                    finish(2 * r + k // PARTS - 2)
                    wait_alone(pool, o_ready, 2 * r + k // PARTS - 1)
                if n + 1 < NSTEPS:
                    lows(4 * r + k + 1, (k + 1) % 2)

            for n in range(6):
                turn(*place(n))
            with pool.Fori(1, NSTEPS // 4 - 2) as r:
                for k in range(2, 6):
                    turn(r, k)
            for n in range(NSTEPS - 6, NSTEPS):
                turn(*place(n))
            finish(CHUNKS - 2)
            pool.wait_ge(o_ready, CHUNKS - 1)
            finish(CHUNKS - 1)

        @block.scalar
        def _(act):
            act.wait_ge(scale_ready, 1)
            for n in SPLIT_ORDER:
                nc.scalar.activation(w_parts[:, n, HIGH, :], raw_weights(keep, n), ACT.Identity,
                                     scale=scale[:, n, 0:1]).then_inc(w_high_ready, 1)
            act.wait_ge(wo_in, 5 * 16)
            nc.scalar.activation(wo_sb[:, :, :], wo_sb[:, :, :], ACT.Identity, scale=scale[:, 2, 3:4]) \
                .then_inc(wo_scaled, 1)

            def take(kind, n, g, buffer, function):
                act.wait_ge(filled[kind], nth(n, NG, g))
                for half in range(2):
                    for par in range(2):
                        src = slot(kind, g)[par * HALF:(par + 1) * HALF, :, half * ST:(half + 1) * ST]
                        i0 = par * PAIRS + g * PROJ_GROUP
                        dst = buffer[half * HALF:(half + 1) * HALF, :, i0:i0 + PROJ_GROUP]
                        last = nc.scalar.activation(dst.rearrange("p s i -> p i s"), src, function)
                last.then_inc(read[kind], 1)

            def take_q(n, g, first):
                if g == 0 and not first:
                    act.wait_ge(q_low_a, nth(n - 1, NG, NG - 1))
                    act.wait_ge(q_low_b, nth(n - 1, NG, NG - 1))
                take("q", n, g, q_f, ACT.Relu)

            def take_v(n, g, first):
                if g == 0 and not first:
                    act.wait_ge(v_low, nth(n - 1, NG, NG - 1))
                take("v", n, g, v_f, ACT.Copy)

            def high_q(n, g, buf):
                act.wait_ge(q_scaled, nth(n, NG, g))
                for half in range(2):
                    rows = slice(half * HALF, (half + 1) * HALF)
                    nc.scalar.activation(heads_of(q_parts[rows, buf, HIGH, :, half, :], g), heads_of(q_f[rows], g),
                                         ACT.Copy).then_inc(q_high, 1)

            def high_v(n, g, buf):
                act.wait_ge(read["v"], nth(n, NG, g))
                nc.scalar.activation(heads_of(v_parts[:, buf, HIGH, :, 0:LH], g), heads_of(v_f, g),
                                     ACT.Copy).then_inc(v_high, 1)

            def prepare(n, buf, first, used_out):
                take_q(n, 0, first)
                take_q(n, 1, first)
                take_v(n, 0, first)
                take_v(n, 1, first)
                if used_out is not None:
                    act.wait_ge(filled["out"], used_out)
                high_q(n, 0, buf)
                high_q(n, 1, buf)
                high_v(n, 0, buf)
                high_v(n, 1, buf)

            def take_y(c, half):
                act.wait_ge(y_filled, nth(c, PARTS, half) + 1)
                act.wait_ge(y_used, c + 1)
                nc.scalar.activation(y_sb[:, half, :], slot("y", 0)[:, 0, :], ACT.Copy).then_inc(y_ready, 1)

            def turn(r, k):
                n = known(r, k)
                if n > PARTS:
                    take_y(2 * r + (k - 1) // PARTS - 1, (k - 1) % PARTS)
                if n + 1 < NSTEPS:
                    step = 4 * r + k + 1
                    prepare(step, (k + 1) % 2, False, nth(step - 2, NT, NT - 1) if n >= 1 else None)

            prepare(0, 0, True, None)
            for n in range(6):
                turn(*place(n))
            with act.Fori(1, NSTEPS // 4 - 1) as r:
                for k in range(2, 6):
                    turn(r, k)
            for n in range(NSTEPS - 2, NSTEPS):
                turn(*place(n))
            take_y(CHUNKS - 2, 1)
            for half in range(PARTS):
                take_y(CHUNKS - 1, half)

        @block.vector
        def _(dve):
            def sum_k(n, g):
                dve.wait_ge(filled["k"], nth(n, NG, g))
                if g == 0:
                    nc.vector.tensor_scalar(k_acc[:, :, :], slot("k", g), 0.0, None, ALU.max).then_inc(read["k"], 1)
                else:
                    dve.wait_ge(read["k"], nth(n, NG, g - 1))
                    nc.vector.scalar_tensor_tensor(out=k_acc[:, :, :], in0=slot("k", g), scalar=0.0,
                                                   in1=k_acc[:, :, :], op0=ALU.max, op1=ALU.add) \
                        .then_inc(read["k"], 1)

            def sum_pairs(n):
                dve.wait_ge(read["k"], nth(n, NG, NG - 1))
                nc.vector.reduce_sum(k_heads[:, :], k_acc[:, :, :].rearrange("p n t -> p t n"), AX_X) \
                    .then_inc(k_heads_ready, 1)

            def scale_q(n):
                dve.wait_ge(filled["sum"], n + 1)
                for half in range(2):
                    rows = slice(half * HALF, (half + 1) * HALF)
                    last = nc.vector.tensor_scalar(k_sum[rows, :], slot("sum", 0)[rows, 0, half * ST:(half + 1) * ST],
                                                   K_SHIFT, None, ALU.mult)
                last.then_inc(read["sum"], 1)
                dve.wait_ge(read["sum"], n + 1)
                for g in range(NG):
                    dve.wait_ge(read["q"], nth(n, NG, g))
                    of_group = heads_of(q_f, g)
                    nc.vector.tensor_tensor(of_group, of_group, k_sum[:, :].unsqueeze(2).unsqueeze(3)
                                            .broadcast_to([P, ST, 2, PROJ_GROUP]), ALU.mult).then_inc(q_scaled, 1)

            def low_q(n, buf, g):
                dve.wait_ge(q_high, nth(n, 2 * NG, 2 * g))
                nc.vector.tensor_tensor(*low_q_operands(buf, g, 0), ALU.subtract).then_inc(q_low_a, 1)

            def add_eps(n, g):
                dve.wait_ge(filled["out"], nth(n, NT, g))
                nc.vector.tensor_scalar(denom[:, g % 2, 0, :], slot("out", g)[:, :, LH], scale[:, 0, 2:3], None,
                                        ALU.add).then_inc(denom_ready, 1)

            def invert(n, g):
                dve.wait_ge(denom_ready, nth(n, NT, g))
                nc.vector.reciprocal(denom[:, g % 2, 1, :], denom[:, g % 2, 0, :]).then_inc(recip_ready, 1)

            def take_out(n, c, k, g, y_used_count):
                if y_used_count is not None:
                    dve.wait_ge(y_filled, y_used_count)
                dve.wait_ge(recip_ready, nth(n, NT, g))
                for half in range(2):
                    for par in range(2):
                        rows = slice(half * HALF, (half + 1) * HALF)
                        s0 = half * CT + (k % PARTS) * ST + g * OUT_GROUP
                        dst = o_s[par * HALF:(par + 1) * HALF, c % 2, :, s0:s0 + OUT_GROUP]
                        last = nc.vector.tensor_tensor(
                            dst.rearrange("p j s -> p s j"), slot("out", g)[rows, :, par * PAIRS:(par + 1) * PAIRS],
                            denom[rows, g % 2, 1, :].unsqueeze(2).broadcast_to([HALF, OUT_GROUP, PAIRS]), ALU.mult)
                last.then_inc(read["out"], 1)

            def turn(r, k):
                n = known(r, k)
                step, buf = 4 * r + k, (k + 1) % 2
                y_count = step - 1 if k % PARTS == 0 and n >= 2 * PARTS else None

                def outs(g):
                    take_out(step, k // PARTS, k, g, y_count if g == 0 else None)

                if n + 1 < NSTEPS:
                    scale_q(step + 1)
                add_eps(step, 0)
                invert(step, 0)
                outs(0)
                add_eps(step, 1)
                invert(step, 1)
                outs(1)
                if n + 2 < NSTEPS:
                    sum_k(step + 2, 0)
                add_eps(step, 2)
                if n + 1 < NSTEPS:
                    low_q(step + 1, buf, 0)
                invert(step, 2)
                if n + 1 < NSTEPS:
                    low_q(step + 1, buf, 1)
                outs(2)
                if n + 2 < NSTEPS:
                    sum_k(step + 2, 1)
                add_eps(step, 3)
                if n + 2 < NSTEPS:
                    sum_pairs(step + 2)
                invert(step, 3)
                outs(3)

            steps = [
                lambda: nc.vector.tensor_scalar(scale[:, :, 1], peak[:, 0:3], 2.0 ** -60, None, ALU.max),
                lambda: nc.vector.tensor_scalar(scale[:, :, 2].bitcast(I32), scale[:, :, 1].bitcast(I32),
                                                0x7F800000, None, ALU.bitwise_and),
                lambda: nc.vector.tensor_scalar(scale[:, :, 3], scale[:, :, 2], 2.0 ** (1 - W_TOP), None, ALU.mult),
                lambda: nc.vector.reciprocal(scale[:, :, 0], scale[:, :, 3])]
            for k, step in enumerate(steps):
                step().then_inc(scale_step, 1)
                dve.wait_ge(scale_step, k + 1)
            dve.nop().then_inc(scale_ready, 1)
            nc.vector.tensor_tensor(scale[:, 0, 1:2], scale[:, 0, 0:1], scale[:, 1, 0:1], ALU.mult) \
                .then_inc(scale_step, 1)
            dve.wait_ge(scale_step, 5)
            nc.vector.tensor_scalar(scale[:, 0, 2:3], scale[:, 0, 1:2], LEPS / LSCALE * K_SHIFT, None, ALU.mult) \
                .then_inc(scale_step, 1)

            def low_weights(k):
                n = SPLIT_ORDER[k]
                dve.wait_ge(w_high_ready, k + 1)
                nc.vector.scalar_tensor_tensor(out=w_parts[:, n, LOW, :], in0=raw_weights(keep, n),
                                               scalar=scale[:, n, 0:1], in1=w_parts[:, n, HIGH, :],
                                               op0=ALU.mult, op1=ALU.subtract).then_inc(w_low_ready, 1)

            low_weights(0)
            low_weights(1)
            for g in range(NG):
                sum_k(0, g)
            sum_pairs(0)
            low_weights(2)
            dve.wait_ge(scale_step, 6)
            scale_q(0)
            for g in range(NG):
                low_q(0, 0, g)
            for g in range(NG):
                sum_k(1, g)
            sum_pairs(1)
            for n in range(6):
                turn(*place(n))
            with dve.Fori(1, NSTEPS // 4 - 1) as r:
                for k in range(2, 6):
                    turn(r, k)
            for n in range(NSTEPS - 2, NSTEPS):
                turn(*place(n))

        @block.tensor
        def _(pe):
            weights = {"q": 0, "k": 1, "v": 2}
            pe.nop().then_inc(y_filled, 1)

            def slot_free(kind, g, r, k):
                turn, i = known(r, k), USES.index((kind, g))
                place = turn * len(USES) + i - SLOTS
                while place >= -2 * len(USES):
                    before, j = USES[place % len(USES)]
                    at = place // len(USES)
                    if happens(before, at):
                        break
                    place -= SLOTS
                else:
                    return
                moved = 4 * r + k + at - turn
                if before == "y":
                    pe.wait_ge(y_ready, moved - PARTS + 1)
                else:
                    pe.wait_ge(read[before], nth(moved + AHEAD[before], PER[before], j))

            def project_group(kind, g, r, k):
                slot_free(kind, g, r, k)
                step = 4 * r + k + AHEAD[kind]
                if g == 0:
                    pe.wait_ge(x_ready, step + 1)
                    if known(r, k) < 0:
                        pe.wait_ge(w_low_ready, SPLIT_ORDER.index(weights[kind]) + 1)
                tokens = x_s[:, (k + AHEAD[kind]) % 4]
                for n in range(PROJ_GROUP):
                    cols = slice((g * PROJ_GROUP + n) * P, (g * PROJ_GROUP + n + 1) * P)
                    for i, (a, b) in enumerate(PASSES):
                        last = nc.tensor.matmul(slot(kind, g)[:, n, :], w_parts[:, weights[kind], a, cols],
                                                tokens[:, b].rearrange("p h s -> p (h s)"),
                                                start=(i == 0), stop=(i == len(PASSES) - 1))
                last.then_inc(filled[kind], 1)

            def out_group(g, r, k):
                slot_free("out", g, r, k)
                for n in range(OUT_GROUP):
                    for i, (a, b) in enumerate(PASSES):
                        last = nc.tensor.matmul(slot("out", g)[:, n, 0:LH + 1],
                                                q_parts[:, k % 2, a, g * OUT_GROUP + n].rearrange("p h i -> p (h i)"),
                                                v_parts[:, k % 2, b, g * OUT_GROUP + n, 0:LH + 1],
                                                start=(i == 0), stop=(i == len(PASSES) - 1))
                last.then_inc(filled["out"], 1)

            def project_out(r, k):
                slot_free("y", 0, r, k)
                half = k % PARTS
                if half == 0:
                    pe.wait_ge(wo_scaled, 1)
                    pe.wait_ge(read["out"], nth(4 * r + k - 1, NT, NT - 1))
                for n in range(PAIRS // PARTS):
                    pair = half * (PAIRS // PARTS) + n
                    last = nc.tensor.matmul(slot("y", 0)[:, 0, :], o_s[:, (k // PARTS - 1) % 2, pair, :],
                                            wo_sb[:, pair, :], start=(n == 0), stop=(n == PAIRS // PARTS - 1))
                last.then_inc(y_filled, 1)

            def turn(r, k):
                n = known(r, k)
                for kind, g in USES:
                    if not happens(kind, n):
                        continue
                    if kind == "sum":
                        if n < 0:
                            pe.wait_ge(consts, 3 + 2 + 8)
                        slot_free("sum", 0, r, k)
                        pe.wait_ge(k_heads_ready, 4 * r + k + 2)
                        nc.tensor.matmul(slot("sum", 0)[:, 0, 0:2 * ST], pair_sum[:, :, :].rearrange("p a d -> p (a d)"),
                                         k_heads[:, :], start=True, stop=True).then_inc(filled["sum"], 1)
                    elif kind == "y":
                        project_out(r, k)
                    elif kind == "out":
                        if g == 0:
                            pe.wait_ge(q_low_a, nth(4 * r + k, NG, NG - 1))
                            pe.wait_ge(q_low_b, nth(4 * r + k, NG, NG - 1))
                            pe.wait_ge(v_low, nth(4 * r + k, NG, NG - 1))
                        out_group(g, r, k)
                    else:
                        project_group(kind, g, r, k)

            turn(0, -2)
            turn(0, -1)
            for n in range(6):
                turn(*place(n))
            with pe.Fori(1, NSTEPS // 4 - 1) as r:
                for k in range(2, 6):
                    turn(r, k)
            for n in range(NSTEPS - 2, NSTEPS + PARTS):
                turn(*place(n))


def rotary_tables():
    import numpy as np
    f32 = np.float32
    half = np.arange(0, FD, 2, dtype=f32)
    inv_freq = (f32(1.0) / np.power(f32(10000.0), half / f32(FD), dtype=f32)).astype(f32)
    t = np.arange(SEQ, dtype=f32)
    freqs = t[:, None] * inv_freq[None, :]
    freqs = np.concatenate([freqs, freqs], axis=-1)
    base = (half + f32(0.4 * FD)) / f32(1.4 * FD)
    power = (t - SEQ // 2) / f32(WIN // 2)
    scale = np.power(base[None, :], power[:, None], dtype=f32)
    scale = np.concatenate([scale, scale], axis=-1)
    sign = np.where(np.arange(FD) < FD // 2, -1.0, 1.0).astype(f32)
    cos, sin = np.cos(freqs).astype(f32), np.sin(freqs).astype(f32) * sign
    q_side = scale * f32(QK_SCALE)
    tables = np.stack([np.stack([cos * q_side, cos / scale]), np.stack([sin * q_side, sin / scale])])
    tables = tables.reshape(2, 2, QT, P, FD).transpose(3, 0, 1, 2, 4)
    return np.ascontiguousarray(tables.reshape(P, -1).astype(f32))


_INS = ["L0_attn_x", "L0_attn_Wq", "L0_attn_Wk", "L0_attn_Wv", "L0_attn_Wo", "L0_attn_bo",
        "L0_ffn_wqkv", "L0_ffn_q_scale", "L0_ffn_k_scale", "L0_ffn_wo", "L0_ffn_ln_g", "L0_ffn_ln_b",
        "L0_ffn_w1", "L0_ffn_b1", "L0_ffn_w2", "L0_ffn_b2"]


def kernel(**inputs):
    import numpy as _np
    import concourse.bacc as _bacc
    from concourse import mybir as _mybir
    from concourse.bass_utils import run_bass_kernel_spmd as _run

    nc = _bacc.Bacc("TRN2", target_bir_lowering=False, num_devices=1)
    arrays, args = {}, []
    for name in _INS:
        a = _np.ascontiguousarray(inputs[name])
        arrays[f"in_{name}"] = a
        args.append(nc.dram_tensor(f"in_{name}", a.shape, _mybir.dt.from_np(a.dtype), kind="ExternalInput").ap())
    tables = rotary_tables()
    arrays["rotary"] = tables
    args.append(nc.dram_tensor("rotary", tables.shape, _mybir.dt.float32, kind="ExternalInput").ap())
    args.append(nc.dram_tensor("out_0", (BATCH, SEQ, DIM), _mybir.dt.float32, kind="ExternalOutput").ap())
    build(nc, *args)
    r = _run(nc, [arrays], core_ids=[0])
    return r.results[0]["out_0"]
```
